# Optimizing a Trainium2 kernel written in Bass

```python
import numpy as np
import jax
import jax.numpy as jnp

def _softmax(x, axis=-1):
    return jax.nn.softmax(x, axis=axis)

def _gelu(x):
    return jax.nn.gelu(x, approximate=True)

def _silu(x):
    return jax.nn.silu(x)

def _sigmoid(x):
    return jax.nn.sigmoid(x)

def _layernorm(x, axis=-1, eps=1e-05):
    m = jnp.mean(x, axis=axis, keepdims=True)
    v = jnp.var(x, axis=axis, keepdims=True)
    return (x - m) / jnp.sqrt(v + eps)

def _scatter_add(tgt, idx, src, axis=0):
    return tgt.at[idx].add(src)

def _segment_sum(src, seg, n):
    return jax.ops.segment_sum(src, seg, n)
kernel_name = 'mk_perceiver_d1_seqx_r8_bc90d6'

def setup_inputs(seed: int=0):
    np.random.seed(seed)
    _w = jnp.asarray

    def _rec_inputs():
        import jax
        import jax.numpy as jnp
        _rk = jax.random.key(seed)
        x = -0.0003929 + 0.9999 * jax.random.normal(jax.random.fold_in(_rk, 1), (1, 128, 256), jnp.float32)
        _lenS = 128 - jax.random.randint(jax.random.fold_in(_rk, 7), (1,), 0, max(1, 128 // 4) + 1, jnp.int32)
        _lenS2 = 2048 - jax.random.randint(jax.random.fold_in(_rk, 8), (1,), 0, max(1, 2048 // 4) + 1, jnp.int32)
        _ctx_1024P = jax.random.normal(jax.random.fold_in(_rk, 11), (1, 16, 128), jnp.float32)
        _ctx_1024c = jax.random.dirichlet(jax.random.fold_in(_rk, 511), 0.3 * jnp.ones((16,), jnp.float32), (1, 2048))
        _ctx_1024t = jnp.einsum('bsk,bkd->bsd', _ctx_1024c, _ctx_1024P)
        _ctx_1024t = _ctx_1024t * jax.lax.rsqrt(jnp.mean(jnp.square(_ctx_1024t)) + 1e-12) * 0.953939
        ctx_1024 = 0.000227908 + 0.99994 * (_ctx_1024t + 0.3 * jax.random.normal(jax.random.fold_in(_rk, 611), (1, 2048, 128), jnp.float32))
        return (x, ctx_1024)
    x, ctx_1024 = _rec_inputs()

    def _L0_xattn_setup():
        import jax, jax.numpy as jnp
        import numpy as np
        EPS = 1e-05

        def rmsnorm(x, g, eps=EPS):
            var = jnp.mean(jnp.square(x), axis=-1, keepdims=True)
            return x * jax.lax.rsqrt(var + eps) * g
        key = jax.random.key(seed)
        ks = jax.random.split(key, 8)
        B, Sq, Skv = (2, 512, 64)
        dim, cdim, H, D = (256, 128, 16, 128)
        inner = H * D
        s = lambda f: 1.0 / np.sqrt(f)
        return {'hidden_states': jax.random.normal(ks[0], (B, Sq, dim), jnp.float32), 'encoder_hidden_states': jax.random.normal(ks[1], (B, Skv, cdim), jnp.float32), 'Wq': jax.random.normal(ks[2], (dim, inner), jnp.float32) * s(dim), 'Wk': jax.random.normal(ks[3], (cdim, inner), jnp.float32) * s(cdim), 'Wv': jax.random.normal(ks[4], (cdim, inner), jnp.float32) * s(cdim), 'Wo': jax.random.normal(ks[5], (inner, dim), jnp.float32) * s(inner), 'gq': jnp.ones((D,), jnp.float32), 'gk': jnp.ones((D,), jnp.float32)}
    _L0_xattn_all = _L0_xattn_setup()
    _L0_xattn_in = {k: v for k, v in _L0_xattn_all.items() if k in ('Wq', 'Wk', 'Wv', 'Wo', 'gq', 'gk')}
    del _L0_xattn_all

    def _L0_attn_setup():
        import jax, jax.numpy as jnp
        import numpy as np
        D_MODEL = 256
        D_INNER = 512
        LN_EPS = 1e-05
        key = jax.random.key(seed)
        k1, k2, k3, k4 = jax.random.split(key, 4)
        B, S = (2, 512)
        x = jax.random.normal(k1, (B, S, D_MODEL), dtype=jnp.float32)
        gamma = jnp.ones((D_MODEL,), dtype=jnp.float32)
        beta = jnp.zeros((D_MODEL,), dtype=jnp.float32)
        W_in = jax.random.normal(k2, (2 * D_INNER, D_MODEL), dtype=jnp.float32) * 0.02
        W_out = jax.random.normal(k3, (D_MODEL, D_INNER), dtype=jnp.float32) * 0.02
        dt_min, dt_max = (0.001, 0.1)
        dt = jax.random.uniform(k4, (D_INNER,), dtype=jnp.float32) * (dt_max - dt_min) + dt_min
        return {'x': x, 'gamma': gamma, 'beta': beta, 'W_in': W_in, 'W_out': W_out, 'dt': dt}
    _L0_attn_all = _L0_attn_setup()
    _L0_attn_in = {k: v for k, v in _L0_attn_all.items() if k in ('gamma', 'beta', 'W_in', 'W_out', 'dt')}
    del _L0_attn_all

    def _L0_ffn_setup():
        import jax, jax.numpy as jnp
        import numpy as np
        TOP_K = 4
        NUM_EXPERTS = 16
        key = jax.random.key(seed)
        ks = jax.random.split(key, 6)
        B, S, H, I, E = (2, 128, 256, 224, NUM_EXPERTS)
        return {'x': jax.random.normal(ks[0], (B, S, H), dtype=jnp.float32), 'router_w': jax.random.normal(ks[1], (E, H), dtype=jnp.float32) * 0.02, 'expert_bias': jnp.zeros((E,), dtype=jnp.float32), 'gate_proj': jax.random.normal(ks[2], (E, H, I), dtype=jnp.float32) * 0.02, 'up_proj': jax.random.normal(ks[3], (E, H, I), dtype=jnp.float32) * 0.02, 'down_proj': jax.random.normal(ks[4], (E, I, H), dtype=jnp.float32) * 0.02}
    _L0_ffn_all = _L0_ffn_setup()
    _L0_ffn_in = {k: v for k, v in _L0_ffn_all.items() if k in ('router_w', 'expert_bias', 'gate_proj', 'up_proj', 'down_proj')}
    del _L0_ffn_all
    return {'x': x, 'ctx_1024': ctx_1024, 'L0_xattn_Wq': _L0_xattn_in['Wq'], 'L0_xattn_Wk': _L0_xattn_in['Wk'], 'L0_xattn_Wv': _L0_xattn_in['Wv'], 'L0_xattn_Wo': _L0_xattn_in['Wo'], 'L0_xattn_gq': _L0_xattn_in['gq'], 'L0_xattn_gk': _L0_xattn_in['gk'], 'L0_attn_gamma': _L0_attn_in['gamma'], 'L0_attn_beta': _L0_attn_in['beta'], 'L0_attn_W_in': _L0_attn_in['W_in'], 'L0_attn_W_out': _L0_attn_in['W_out'], 'L0_attn_dt': _L0_attn_in['dt'], 'L0_ffn_router_w': _L0_ffn_in['router_w'], 'L0_ffn_expert_bias': _L0_ffn_in['expert_bias'], 'L0_ffn_gate_proj': _L0_ffn_in['gate_proj'], 'L0_ffn_up_proj': _L0_ffn_in['up_proj'], 'L0_ffn_down_proj': _L0_ffn_in['down_proj']}

def reference(x, ctx_1024, L0_xattn_Wq, L0_xattn_Wk, L0_xattn_Wv, L0_xattn_Wo, L0_xattn_gq, L0_xattn_gk, L0_attn_gamma, L0_attn_beta, L0_attn_W_in, L0_attn_W_out, L0_attn_dt, L0_ffn_router_w, L0_ffn_expert_bias, L0_ffn_gate_proj, L0_ffn_up_proj, L0_ffn_down_proj):
    import jax
    import jax.numpy as jnp

    def _L0_xattn_ref(hidden_states, encoder_hidden_states, Wq, Wk, Wv, Wo, gq, gk):
        import jax, jax.numpy as jnp
        import numpy as np
        EPS = 1e-05

        def rmsnorm(x, g, eps=EPS):
            var = jnp.mean(jnp.square(x), axis=-1, keepdims=True)
            return x * jax.lax.rsqrt(var + eps) * g
        B, Sq, _ = hidden_states.shape
        Skv = encoder_hidden_states.shape[1]
        D = gq.shape[0]
        H = Wq.shape[1] // D
        scale = 1.0 / np.sqrt(D)
        q = (hidden_states @ Wq).reshape(B, Sq, H, D)
        k = (encoder_hidden_states @ Wk).reshape(B, Skv, H, D)
        v = (encoder_hidden_states @ Wv).reshape(B, Skv, H, D)
        q = rmsnorm(q, gq)
        k = rmsnorm(k, gk)
        scores = jnp.einsum('bqhd,bkhd->bhqk', q, k) * scale
        attn = jax.nn.softmax(scores, axis=-1)
        out = jnp.einsum('bhqk,bkhd->bqhd', attn, v)
        out = out.reshape(B, Sq, H * D)
        return out @ Wo

    def _L0_attn_ref(x, gamma, beta, W_in, W_out, dt):
        import jax, jax.numpy as jnp
        import numpy as np
        D_MODEL = 256
        D_INNER = 512
        LN_EPS = 1e-05
        identity = x
        mu = jnp.mean(x, axis=-1, keepdims=True)
        var = jnp.mean(jnp.square(x - mu), axis=-1, keepdims=True)
        xn = (x - mu) * jax.lax.rsqrt(var + LN_EPS) * gamma + beta
        projected = jnp.einsum('bsd,ed->bse', xn, W_in)
        z, gate = jnp.split(projected, 2, axis=-1)
        z_gated = z * jax.nn.sigmoid(jnp.clip(z, -15.0, 15.0))
        dt_weights = jax.nn.softmax(-dt)
        z_temporal = z_gated * dt_weights
        output = z_temporal * jax.nn.silu(jnp.clip(gate, -15.0, 15.0))
        output = jnp.einsum('bse,de->bsd', output, W_out)
        return output + identity

    def _L0_ffn_ref(x, router_w, expert_bias, gate_proj, up_proj, down_proj):
        import jax, jax.numpy as jnp
        import numpy as np
        TOP_K = 4
        NUM_EXPERTS = 16
        logits = jnp.einsum('bsh,eh->bse', x, router_w) + expert_bias
        scores = jax.nn.softmax(logits, axis=-1)
        top_w, top_idx = jax.lax.top_k(scores, TOP_K)
        top_w = top_w / jnp.sum(top_w, axis=-1, keepdims=True)
        g = jnp.einsum('bsh,khe->bske', x, gate_proj)
        u = jnp.einsum('bsh,khe->bske', x, up_proj)
        act = jax.nn.silu(g) * u
        out = jnp.einsum('bske,keh->bskh', act, down_proj)
        sel = jnp.take_along_axis(out, top_idx[..., None], axis=2)
        return jnp.sum(sel * top_w[..., None], axis=2)
    x = x + _L0_xattn_ref(_layernorm(x, axis=-1), ctx_1024, L0_xattn_Wq, L0_xattn_Wk, L0_xattn_Wv, L0_xattn_Wo, L0_xattn_gq, L0_xattn_gk)
    x = x + _L0_attn_ref(_layernorm(x, axis=-1), L0_attn_gamma, L0_attn_beta, L0_attn_W_in, L0_attn_W_out, L0_attn_dt)
    x = x + _L0_ffn_ref(_layernorm(x, axis=-1), L0_ffn_router_w, L0_ffn_expert_bias, L0_ffn_gate_proj, L0_ffn_up_proj, L0_ffn_down_proj)
    return x

_drawn_inputs = setup_inputs


def setup_inputs(seed=0):
    import zlib

    import numpy as np

    out = dict(_drawn_inputs(seed))
    spreads = {'L0_xattn_gq': (1.0, 0.2),
     'L0_xattn_gk': (1.0, 0.2),
     'L0_attn_gamma': (1.0, 0.6),
     'L0_attn_beta': (0.0, 0.8),
     'L0_ffn_expert_bias': (0.0, 0.8)}
    factors = {'L0_attn_W_in': 8.0,
     'L0_attn_W_out': 8.0,
     'L0_attn_dt': 27.295,
     'L0_ffn_router_w': 8.0,
     'L0_ffn_gate_proj': 8.0,
     'L0_ffn_up_proj': 8.0,
     'L0_ffn_down_proj': 8.0}
    for name, (base, spread) in spreads.items():
        noise = np.random.default_rng([zlib.crc32(name.encode()), seed]).standard_normal(out[name].shape)
        drawn = base * np.exp(spread * noise) if base else spread * noise
        out[name] = jnp.asarray(drawn.astype(out[name].dtype))
    for name, factor in factors.items():
        out[name] = (out[name] * factor).astype(out[name].dtype)
    return out
```

```python
import concourse.bass as bass
from concourse import mybir

F32 = mybir.dt.float32
F32R = mybir.dt.float32r
I32 = mybir.dt.int32
ALU = mybir.AluOpType
ACT = mybir.ActivationFunctionType
AX = mybir.AxisListType

P = 128
EPS = 1e-5


def perceiver_layer(nc, x, ctx, Wq, Wk, Wv, Wo, gq, gk, gamma, beta, W_in, W_out, dt, router_w,
                    expert_bias, gate_proj, up_proj, down_proj, out):
    T, DM = x.shape[1], x.shape[2]
    NKEY, C = ctx.shape[1], ctx.shape[2]
    D = gq.shape[0]
    H = Wq.shape[1] // D
    KT = NKEY // P
    GH = 4
    G = H // GH
    BANK = 512
    NC = NKEY // BANK
    DI = dt.shape[0]
    E, I = gate_proj.shape[0], gate_proj.shape[2]
    IH = I // 2
    DA = DM // P
    TOP_K = 4

    UNITS = KT // 2
    S_AT = 2 * UNITS
    C_AT = S_AT + UNITS + 1
    SLOTS = C_AT + G * UNITS
    R_TURN = 3
    V_AT = 3

    KB = 1024
    base = (nc.sbuf_base + 31) // 32 * 32

    def at(name, shape, kb, dtype=F32):
        return nc.alloc_sbuf_tensor_at(name, shape, dtype, offset=base + int(kb * KB))

    ctx_hi = at("ctx_hi", [P, KT, C], 0, F32R)
    ctx_lo = at("ctx_lo", [P, KT, C], 8, F32R)
    ctxT_hi = at("ctxT_hi", [C, NKEY], 16, F32R)
    ctxT_lo = at("ctxT_lo", [C, NKEY], 24, F32R)
    wk_hi = at("wk_hi", [C, H * D], 32, F32R)
    wk_lo = at("wk_lo", [C, H * D], 40, F32R)
    u_hi = at("u_hi", [C, H, T], 48, F32R)
    u_lo = at("u_lo", [C, H, T], 56, F32R)
    prob = [at(f"prob{i}", [T, GH, NKEY], 64 + 32 * i) for i in range(2)]
    rbc = [at(f"rbc{i}", [P, NKEY], 128 + 8 * i) for i in range(2)]
    rrow = at("rrow", [P, NKEY], 144)
    pT_hi = at("pT_hi", [P, 2, BANK], 152, F32R)
    pT_lo = at("pT_lo", [P, 2, BANK], 156, F32R)
    wv = at("wv", [C, H * D], 160)
    wo = at("wo", [D, H, DM], 168)
    w_inT = at("w_inT", [P, DA, 2 * DI], 184)
    w_outT = at("w_outT", [P, DI // P, DM], 192)
    small = [196.0]

    def tiny(name, shape, dtype=F32):
        n = 4
        for d in shape[1:]:
            n *= d
        t = at(name, shape, small[0], dtype)
        small[0] += (n + 31) // 32 * 32 / KB
        return t

    wq_sb = at("wq_sb", [P, DA, H * D], 64)
    q_sb = at("q_sb", [T, H * D], 80)
    qT = at("qT", [D, H, T], 88)
    wk_sb = at("wk_sb", [C, H * D], 96)
    wkT = at("wkT", [D, H, C], 104)
    w_in_sb = at("w_in_sb", [P, 2 * DI // P, DM], 112)
    w_out_sb = at("w_out_sb", [P, DA, DI], 120)
    junk_a = at("junk_a", [P, 4, D], 124)
    ctx_sb = at("ctx_sb", [P, KT, C], 128)
    oT = at("oT", [C, GH * T], 32)
    vo_sb = at("vo_sb", [T, GH * D], 34)
    voT = at("voT", [D, GH, T], 36)
    dt_sb = at("dt_sb", [P, DI], 38)
    guw = at("guw", [P, E, DA, 2 * I], 64)
    dww = at("dww", [IH, E, 2, DM], 120)
    x1 = at("x1", [T, DM], 0)
    y1 = at("y1", [T, DM], 1)
    s1 = at("s1", [T, DM], 2)
    xn2 = at("xn2", [T, DM], 3)
    x2 = at("x2", [T, DM], 4)
    xm = at("xm", [T, DM], 5)
    x2T = at("x2T", [P, DA, T], 6)
    xmT = at("xmT", [P, DA, T], 7)
    zc = at("zc", [T, 2, DI], 8)
    sg = at("sg", [T, 2, DI], 12)
    zz = at("zz", [T, DI], 16)
    gg = at("gg", [T, DI], 18)
    oo = at("oo", [T, DI], 20)
    ooT = at("ooT", [P, DI // P, T], 22)
    silu_g = at("silu_g", [T, 2, I], 24)
    acts = at("acts", [T, 2, I], 26)
    actT = at("actT", [IH, 2, 2, T], 28)
    x3 = at("x3", [T, DM], 30)

    ident = tiny("ident", [P, P])
    x_sb = tiny("x_sb", [T, DM])
    xn = tiny("xn", [T, DM])
    xnT = tiny("xnT", [P, DA, T])
    ssq = tiny("ssq", [P, G, GH, KT])
    bn = tiny("bn", [P, GH, UNITS, 6])
    rk = tiny("rk", [P, G, GH, KT])
    ta = tiny("ta", [P, GH * KT])
    tb = tiny("tb", [P, GH * KT])
    rkT = tiny("rkT", [GH * KT, P])
    qsq = tiny("qsq", [T, H])
    rq = tiny("rq", [T, H])
    gcol = tiny("gcol", [D, 2])
    gg_s = tiny("gg_s", [D, 1])
    gamma_c = tiny("gamma_c", [P, DA])
    beta_c = tiny("beta_c", [P, DA])
    stat = tiny("stat", [T, 6])
    mv = tiny("mv", [T, 2])
    rstd = tiny("rstd", [T, 1])
    mhalf = tiny("mhalf", [P, 1])
    smax = tiny("smax", [T, H, NC])
    nmax = tiny("nmax", [T, H])
    pmax = tiny("pmax", [T, H])
    psum_ = tiny("psum_", [T, H])
    rs = tiny("rs", [T, H])
    rw_sb = tiny("rw_sb", [E, DM])
    rwT = tiny("rwT", [P, DA, E])
    bias_bc = tiny("bias_bc", [P, E])
    dstat = tiny("dstat", [P, 4])
    lg = tiny("lg", [T, E])
    ex = tiny("ex", [T, E])
    rank = tiny("rank", [T, E])
    top = tiny("top", [T, E])
    wgt = tiny("wgt", [T, E])
    lstat = tiny("lstat", [T, 4])
    cmp_a = at("cmp_a", [T, E, E], 41)
    cmp_b = at("cmp_b", [T, E, E], 42)
    before = at("before", [P, E, E], 40)
    assert base + small[0] * KB <= nc.sbuf_usable_end, small[0]

    bank = [nc.alloc_psum_tensor(f"bank{i}", [P, BANK], F32) for i in range(8)]
    k_bank = bank[0:2]
    s_bank = bank[2:5]
    t_bank = bank[5:7]
    c_bank = bank[7]
    q_bank = [bank[2], bank[3], bank[4], bank[5]]
    pre_bank = [bank[6], bank[7]]
    v_bank, y_bank = k_bank

    def sem(name):
        return nc.alloc_semaphore(name)

    ld_ctx, ld_wk, ld_x, ld_wq, ld_g, ld_win, ld_wout, ld_gb = map(sem, (
        "ld_ctx", "ld_wk", "ld_x", "ld_wq", "ld_g", "ld_win", "ld_wout", "ld_gb"))
    ld_rw, ld_bias, ld_wv, ld_wo, ld_dt = map(sem, ("ld_rw", "ld_bias", "ld_wv", "ld_wo", "ld_dt"))
    ld_exp = [sem(f"ld_exp{i}") for i in range(4)]
    ident_made, mhalf_made, before_made = map(sem, ("ident_made", "mhalf_made", "before_made"))
    ctx_hi_done, ctx_lo_done = map(sem, ("ctx_hi_done", "ctx_lo_done"))
    pre_t, pre_a, pre_v = map(sem, ("pre_t", "pre_a", "pre_v"))
    wk_hi_done, wk_lo_done = map(sem, ("wk_hi_done", "wk_lo_done"))
    k_done, k_sq, k_bn, rk_ready, rk_turned, rkT_ready, rrow_ld, rbc_ready = map(sem, (
        "k_done", "k_sq", "k_bn", "rk_ready", "rk_turned", "rkT_ready", "rrow_ld", "rbc_ready"))
    var_ready, rstd_ready, ln_ready = map(sem, ("var_ready", "rstd_ready", "ln_ready"))
    q_done, q_sq, q_norm, u_done = map(sem, ("q_done", "q_sq", "q_norm", "u_done"))
    s_done, sr_done, nmax_ready, p_ready = map(sem, ("s_done", "sr_done", "nmax_ready", "p_ready"))
    t_done, hi_done, lo_done, c_done, oT_ready = map(sem, (
        "t_done", "hi_done", "lo_done", "c_done", "oT_ready"))
    vo_done, vo_ready, voT_done, voT_ready, y_done = map(sem, (
        "vo_done", "vo_ready", "voT_done", "voT_ready", "y_done"))
    t2, a2, pr_done, clip_done, sig_done, oo_ready, ooT_done, ooT_ready, mo_done = map(sem, (
        "t2", "a2", "pr_done", "clip_done", "sig_done", "oo_ready", "ooT_done", "ooT_ready", "mo_done"))
    dt_neg, dt_exp, lg_done, lg_max, lg_exp = map(sem, ("dt_neg", "dt_exp", "lg_done", "lg_max", "lg_exp"))
    gu_done, silu_done, act_ready, at_done, at_ready, dn_done, x3_ready, stored = map(sem, (
        "gu_done", "silu_done", "act_ready", "at_done", "at_ready", "dn_done", "x3_ready", "stored"))
    dve_seq, gg_ready, rq_ready = map(sem, ("dve_seq", "gg_ready", "rq_ready"))

    CTX0, XN, WK0, QT0, U0, WIN0, WOUT0, RW0 = 0, 4, 5, 9, 13, 17, 21, 23
    PRE_AT = {XN: 3, WK0: 1, QT0: 10, U0: 12, WIN0: 13, WOUT0: 14, RW0: 14}

    block = nc.Block()
    with block:
        def load_experts(eng, lo, hi, done):
            gv = gate_proj.rearrange("e (a p) i -> p e a i", p=P)
            uv = up_proj.rearrange("e (a p) i -> p e a i", p=P)
            for a in range(DA):
                eng.dma_start(guw[:, lo:hi, a, 0:I], gv[:, lo:hi, a, :]).then_inc(done, 16)
                eng.dma_start(guw[:, lo:hi, a, I:2 * I], uv[:, lo:hi, a, :]).then_inc(done, 16)

        CTX_V = 4

        def rstd_of(pool, n):
            pool.wait_ge(var_ready, n + 1)
            pool.tensor_tensor(out=rstd[:, :], in0=mv[:, 1:2], in1=mhalf[0:T, :], op=ALU.pow).then_inc(rstd_ready, 1)

        def acts_turned(act, e):
            act.wait_ge(at_done, e + 1)
            if e >= 2:
                act.wait_ge(dn_done, e - 1)
            nc.scalar.activation(actT[:, e % 2, :, :].rearrange("p a t -> p (a t)"), bank[4 + e % 2][0:IH, 0:2 * T],
                                 ACT.Copy).then_inc(at_ready, 1)

        @block.sync
        def _(sp):
            ctx_v = ctx[0, :, :].rearrange("(p t) c -> p t c", t=KT)
            for i in range(2):
                sp.dma_start(ctx_sb[:, 8 * i:8 * i + 8, :], ctx_v[:, 8 * i:8 * i + 8, :]).then_inc(ld_ctx, 16)
                sp.wait_ge(ld_ctx, 16 * (i + 1))
            sp.dma_start(x_sb[:, :], x[0, :, :]).then_inc(ld_x, 16)
            sp.dma_start(wq_sb[:, :, :], Wq.rearrange("(a p) n -> p a n", p=P)).then_inc(ld_wq, 16)
            sp.dma_start(gcol[:, 0:1], gq.rearrange("(p a) -> p a", a=1)).then_inc(ld_g, 16)
            sp.dma_start(gcol[:, 1:2], gk.rearrange("(p a) -> p a", a=1)).then_inc(ld_g, 16)
            sp.dma_start(w_in_sb[:, :, :], W_in.rearrange("(j p) d -> p j d", p=P)).then_inc(ld_win, 16)
            sp.dma_start(w_out_sb[:, :, :], W_out.rearrange("(a p) e -> p a e", p=P)).then_inc(ld_wout, 16)
            sp.dma_start(rw_sb[:, :], router_w).then_inc(ld_rw, 16)
            sp.dma_start(wv[:, :], Wv).then_inc(ld_wv, 16)
            sp.dma_start(wo[:, :, :], Wo.rearrange("(h d) n -> d h n", d=D)).then_inc(ld_wo, 16)
            for a in range(DA):
                for dst, src in ((gamma_c, gamma), (beta_c, beta)):
                    sp.dma_start(dst[:, a:a + 1], src[P * a:P * a + P].rearrange("(p o) -> p o", o=1)).then_inc(ld_gb, 16)
            sp.dma_start(bias_bc[:, :], expert_bias.rearrange("(a e) -> a e", a=1).to_broadcast([P, E])).then_inc(ld_bias, 16)
            for g in range(G):
                sp.wait_ge(rkT_ready, g + 1)
                if g > 0:
                    sp.wait_ge(rbc_ready, GH * g)
                for j in range(GH):
                    sp.dma_start(rrow[32 * j:32 * j + 1, :].rearrange("a (t p) -> a t p", p=P),
                                 rkT[KT * j:KT * j + KT, :]).then_inc(rrow_ld, 16)
            sp.wait_ge(k_done, G * KT)
            sp.dma_start(dt_sb[:, :], dt.rearrange("(a e) -> a e", a=1).to_broadcast([P, DI])).then_inc(ld_dt, 16)
            sp.wait_ge(t_done, 3 * KT)
            for n, (lo, hi) in enumerate(((0, 4), (4, 9))):
                load_experts(sp, lo, hi, ld_exp[n])
            sp.wait_ge(t_done, 4 * KT)
            sp.wait_ge(sr_done, H * NC)
            load_experts(sp, 9, 16, ld_exp[2])
            down_v = down_proj.rearrange("e (a p) d -> p e a d", p=IH)
            for a in range(2):
                sp.dma_start(dww[:, :, a, :], down_v[:, :, a, :]).then_inc(ld_exp[3], 16)
            sp.wait_ge(x3_ready, 1)
            sp.dma_start(out[0, :, :], x3[:, :]).then_inc(stored, 16)
            sp.wait_ge(stored, 16)

        def halved(n):
            return n + 1 if n < XN else n - U0 + 5 if U0 <= n < WIN0 else 0

        @block.gpsimd
        def _(pool):
            pool.memset(ident[:, :], 0.0).then_inc(ident_made, 1)
            pool.wait_ge(ident_made, 1)
            pool.affine_select(out=ident[:, :], in_=ident[:, :], compare_op=ALU.not_equal, fill=1.0, base=0,
                               pattern=[[-1, P]], channel_multiplier=1).then_inc(ident_made, 1)
            pool.memset(mhalf[:, :], -0.5).then_inc(mhalf_made, 1)
            for i in range(4):
                pool.wait_ge(ld_ctx, 16 * (i // 2 + 1))
                t0, t1 = 4 * i, 4 * i + 4
                pool.tensor_scalar(out=ctx_hi[:, t0:t1, :], in0=ctx_sb[:, t0:t1, :], scalar1=1.0, scalar2=0.0,
                                   op0=ALU.mult, op1=ALU.add).then_inc(ctx_hi_done, 1)
                pool.wait_ge(ctx_hi_done, i + 1)
                pool.tensor_tensor(out=ctx_lo[:, t0:t1, :], in0=ctx_sb[:, t0:t1, :],
                                   in1=ctx_hi[:, t0:t1, :].bitcast(F32), op=ALU.subtract).then_inc(ctx_lo_done, 1)
                if i == 1:
                    rstd_of(pool, 0)
            for h in range(H):
                g, j = h // GH, h % GH
                pool.wait_ge(rrow_ld, 16 * GH * (g + 1))
                if h >= 2:
                    pool.wait_ge(sr_done, NC * (h - 1))
                if h < 2:
                    pool.wait_ge(pre_v, CTX_V)
                    pool.wait_ge(ctx_lo_done, 4)
                pool.partition_broadcast(rbc[h % 2][:, :], rrow[32 * j:32 * j + 1, :]).then_inc(rbc_ready, 1)
            pool.wait_ge(k_done, G * KT)
            pool.memset(before[:, :, :], 1.0).then_inc(before_made, 1)
            pool.wait_ge(before_made, 1)
            pool.affine_select(out=before[:, :, :], in_=before[:, :, :], compare_op=ALU.is_gt, fill=0.0, base=0,
                               pattern=[[1, E], [-1, E]], channel_multiplier=0).then_inc(before_made, 1)
            for n in range(1, 4):
                rstd_of(pool, n)

        @block.tensor
        def _(pe):
            def turn(n, pieces, need=None):
                if n >= 2:
                    pe.wait_ge(pre_a, n - 1)
                    if halved(n - 2):
                        pe.wait_ge(pre_v, halved(n - 2))
                for i, emit in enumerate(pieces):
                    last = emit(pre_bank[n % 2], i)
                last.then_inc(pre_t, 1)

            def turned(src, rows=P):
                cols = src.shape[1]
                return lambda b, i: nc.tensor.transpose(b[0:cols, P * i:P * i + rows], src, ident[0:rows, 0:rows])

            pe.wait_ge(ident_made, 2)
            for n in range(4):
                pe.wait_ge(ld_ctx, 16 * (n // 2 + 1))
                turn(CTX0 + n, [turned(ctx_sb[:, 4 * n + i, :]) for i in range(4)])

            def three_passes(dst, w_hi, w_lo, m_hi, m_lo):
                nc.tensor.matmul(dst, w_hi, m_hi, start=True, stop=False)
                nc.tensor.matmul(dst, w_hi, m_lo, start=False, stop=False)
                return nc.tensor.matmul(dst, w_lo, m_hi, start=False, stop=True)

            def k_unit(s):
                g = s // UNITS
                if s % UNITS == R_TURN and g > 0:
                    turn_norms(g - 1)
                for t in (2 * (s % UNITS), 2 * (s % UNITS) + 1):
                    n = KT * g + t
                    if n // 2 > 0:
                        pe.wait_ge((k_sq, k_bn)[t % 2], n // 2)
                    if g > 0 and t == 2 * R_TURN:
                        pe.wait_ge(rkT_ready, g)
                    if t == 0:
                        pe.wait_ge(wk_lo_done, g + 1)
                        pe.wait_ge(wk_hi_done, g + 1)
                    if g == 0 and t % 4 == 0:
                        pe.wait_ge(pre_v, t // 4 + 1)
                        pe.wait_ge(pre_a, t // 4 + 1)
                    c0 = slice(t * P, t * P + P)
                    w0 = slice(g * BANK, g * BANK + BANK)
                    three_passes(k_bank[t % 2][:, :], ctxT_hi[:, c0], ctxT_lo[:, c0],
                                 wk_hi[:, w0], wk_lo[:, w0]).then_inc(k_done, 1)

            def turn_norms(g):
                pe.wait_ge(rk_ready, g + 1)
                pe.wait_ge(k_sq, min(UNITS * (g + 1) + R_TURN, UNITS * G))
                nc.tensor.transpose(k_bank[0][0:GH * KT, 0:P], rk[:, g, :, :].rearrange("p h t -> p (h t)"),
                                    ident[:, :]).then_inc(rk_turned, 1)

            def q_products():
                pe.wait_ge(ld_wq, 16)
                pe.wait_ge(pre_a, XN + 1)
                for n in range(4):
                    for a in range(DA):
                        last = nc.tensor.matmul(q_bank[n][:, :], xnT[:, a, :], wq_sb[:, a, n * BANK:n * BANK + BANK],
                                                start=(a == 0), stop=(a == DA - 1))
                    last.then_inc(q_done, 1)

            def before_scores(s):
                if s == 1:
                    pe.wait_ge(ln_ready, 1)
                    turn(XN, [turned(xn[:, P * a:P * a + P]) for a in range(DA)])
                if s == 2:
                    for n in range(4):
                        turn(WK0 + n, [turned(wk_sb[:, P * h:P * h + P]) for h in range(4 * n, 4 * n + 4)])
                if s == 6:
                    q_products()
                if s == 10:
                    for n in range(4):
                        pe.wait_ge(q_norm, n + 1)
                        turn(QT0 + n, [turned(q_sb[:, P * h:P * h + P]) for h in range(4 * n, 4 * n + 4)])
                if s == 12:
                    pe.wait_ge(pre_a, QT0 + 4)
                    for n in range(4):
                        turn(U0 + n, [
                            lambda b, i, h=h: nc.tensor.matmul(b[:, P * i:P * i + T], wkT[:, h, :], qT[:, h, :],
                                                               start=True, stop=True)
                            for h in range(4 * n, 4 * n + 4)])
                if s == 14:
                    pe.wait_ge(ld_win, 16)
                    for n in range(4):
                        turn(WIN0 + n, [turned(w_in_sb[:, 2 * n + i // 2, P * (i % 2):P * (i % 2) + P])
                                        for i in range(4)])
                    pe.wait_ge(ld_wout, 16)
                    for n in range(2):
                        turn(WOUT0 + n, [turned(w_out_sb[:, i % 2, P * (2 * n + i // 2):P * (2 * n + i // 2) + P])
                                         for i in range(4)])
                    pe.wait_ge(ld_rw, 16)
                    turn(RW0, [turned(rw_sb[:, P * a:P * a + P], rows=E) for a in range(DA)])

            def s_chunk(u, c2):
                h, c = u // 2, 2 * (u % 2) + c2
                n = NC * h + c
                if n == 0:
                    pe.wait_ge(pre_v, halved(U0 + 3))
                    pe.wait_ge(pre_a, RW0 + 1)
                    pe.wait_ge(q_norm, 4)
                if n >= 3:
                    pe.wait_ge(sr_done, n - 2)
                c0 = slice(c * BANK, c * BANK + BANK)
                three_passes(s_bank[n % 3][:, :], u_hi[:, h, :], u_lo[:, h, :],
                             ctxT_hi[:, c0], ctxT_lo[:, c0]).then_inc(s_done, 1)

            def turn_probs(m):
                g, kt = m // KT, m % KT
                if kt == 0:
                    pe.wait_ge(p_ready, GH * (g + 1))
                if m >= 2:
                    pe.wait_ge(lo_done, m - 1)
                for j in range(GH):
                    last = nc.tensor.transpose(t_bank[m % 2][:, P * j:P * j + T],
                                               prob[g % 2][:, j, kt * P:kt * P + P], ident[:, :])
                last.then_inc(t_done, 1)

            def times_ctx(m):
                g, kt = m // KT, m % KT
                if kt == 0 and g > 0:
                    pe.wait_ge(oT_ready, g)
                if m == 0:
                    pe.wait_ge(ctx_lo_done, 4)
                pe.wait_ge(lo_done, m + 1)
                pe.wait_ge(hi_done, m + 1)
                hi, lo = pT_hi[:, m % 2, :], pT_lo[:, m % 2, :]
                nc.tensor.matmul(c_bank[:, :], ctx_hi[:, kt, :], hi, start=(kt == 0), stop=False)
                nc.tensor.matmul(c_bank[:, :], ctx_lo[:, kt, :], hi, start=False, stop=False)
                nc.tensor.matmul(c_bank[:, :], ctx_hi[:, kt, :], lo, start=False,
                                 stop=(kt == KT - 1)).then_inc(c_done, 1)

            def value_and_out(g):
                pe.wait_ge(oT_ready, g + 1)
                if g == 0:
                    pe.wait_ge(ld_wv, 16)
                    pe.wait_ge(ld_wo, 16)
                    pe.wait_ge(k_sq, UNITS * G)
                    pe.wait_ge(k_bn, UNITS * G)
                    pe.wait_ge(rkT_ready, G)
                for j in range(GH):
                    h = GH * g + j
                    last = nc.tensor.matmul(v_bank[:, D * j:D * j + D], oT[:, T * j:T * j + T], wv[:, D * h:D * h + D],
                                            start=True, stop=True)
                last.then_inc(vo_done, 1)
                pe.wait_ge(vo_ready, g + 1)
                for j in range(GH):
                    last = nc.tensor.transpose(v_bank[:, T * j:T * j + T], vo_sb[:, D * j:D * j + D], ident[:, :])
                last.then_inc(voT_done, 1)
                pe.wait_ge(voT_ready, g + 1)
                for j in range(GH):
                    h = GH * g + j
                    last = nc.tensor.matmul(y_bank[:, 0:DM], voT[:, j, :], wo[:, h, :],
                                            start=(h == 0), stop=(h == H - 1))
                last.then_inc(y_done, 1)

            for s in range(SLOTS):
                k, su, cu = s, s - S_AT, s - C_AT
                before_scores(s)
                for half in range(2):
                    if 0 <= cu < G * UNITS:
                        m = 2 * cu + half
                        turn_probs(m)
                        if m > 0:
                            times_ctx(m - 1)
                    if 0 <= su < G * UNITS:
                        s_chunk(su, half)
                if k < G * UNITS:
                    k_unit(k)
                if s == G * UNITS + R_TURN:
                    turn_norms(G - 1)
                if cu >= UNITS and cu % UNITS == V_AT:
                    value_and_out(cu // UNITS - 1)
            times_ctx(G * KT - 1)
            value_and_out(G - 1)

            pe.wait_ge(ln_ready, 3)
            for a in range(DA):
                last = nc.tensor.transpose(bank[2][:, P * a:P * a + T], xn2[:, P * a:P * a + P], ident[:, :])
            last.then_inc(t2, 1)
            pe.wait_ge(a2, 1)
            for n in range(2):
                for a in range(DA):
                    last = nc.tensor.matmul(bank[3 + n][:, :], x2T[:, a, :], w_inT[:, a, n * DI:n * DI + DI],
                                            start=(a == 0), stop=(a == DA - 1))
                last.then_inc(pr_done, 1)
            pe.wait_ge(oo_ready, 1)
            for n in range(DI // P):
                last = nc.tensor.transpose(bank[5][:, P * n:P * n + T], oo[:, P * n:P * n + P], ident[:, :])
            last.then_inc(ooT_done, 1)
            pe.wait_ge(ooT_ready, 1)
            for n in range(DI // P):
                last = nc.tensor.matmul(bank[6][:, 0:DM], ooT[:, n, :], w_outT[:, n, :],
                                        start=(n == 0), stop=(n == DI // P - 1))
            last.then_inc(mo_done, 1)

            pe.wait_ge(ln_ready, 4)
            for a in range(DA):
                last = nc.tensor.transpose(bank[7][:, P * a:P * a + T], xm[:, P * a:P * a + P], ident[:, :])
            last.then_inc(t2, 1)
            pe.wait_ge(a2, 2)
            for a in range(DA):
                last = nc.tensor.matmul(bank[0][:, 0:E], xmT[:, a, :], rwT[:, a, :], start=(a == 0), stop=(a == DA - 1))
            last.then_inc(lg_done, 1)

            def gate_up(e):
                if e == 0:
                    pe.wait_ge(ld_exp[0], 64)
                if e == 4:
                    pe.wait_ge(ld_exp[1], 64)
                if e == 9:
                    pe.wait_ge(ld_exp[2], 64)
                if e >= 2:
                    pe.wait_ge(act_ready, e - 1)
                for a in range(DA):
                    last = nc.tensor.matmul(bank[2 + e % 2][:, 0:2 * I], xmT[:, a, :], guw[:, e, a, :],
                                            start=(a == 0), stop=(a == DA - 1))
                last.then_inc(gu_done, 1)

            def turn_acts(e):
                pe.wait_ge(act_ready, e + 1)
                if e >= 2:
                    pe.wait_ge(at_ready, e - 1)
                for a in range(2):
                    last = nc.tensor.transpose(bank[4 + e % 2][0:IH, T * a:T * a + T], acts[:, e % 2, IH * a:IH * a + IH],
                                               ident[:, :])
                last.then_inc(at_done, 1)

            def down(e):
                pe.wait_ge(at_ready, e + 1)
                if e == 0:
                    pe.wait_ge(ld_exp[3], 32)
                for a in range(2):
                    last = nc.tensor.matmul(bank[7][:, 0:DM], actT[:, e % 2, a, :], dww[:, e, a, :],
                                            start=(e == 0 and a == 0), stop=(e == E - 1 and a == 1))
                last.then_inc(dn_done, 1)

            for e in range(E + 2):
                if e < E:
                    gate_up(e)
                if 1 <= e <= E:
                    turn_acts(e - 1)
                if e >= 2:
                    down(e - 2)

        @block.scalar
        def _(act):
            for i in range(4):
                act.dma_start(wk_sb[:, i * BANK:i * BANK + BANK], Wk[:, i * BANK:i * BANK + BANK]).then_inc(ld_wk, 16)
                act.wait_ge(ld_wk, 16 * (i + 1))
                nc.scalar.activation(wk_hi[:, i * BANK:i * BANK + BANK], wk_sb[:, i * BANK:i * BANK + BANK],
                                     ACT.Copy).then_inc(wk_hi_done, 1)
                act.wait_ge(pre_t, i + 1)
                nc.scalar.activation(ctxT_hi[:, i * BANK:i * BANK + BANK], pre_bank[i % 2][:, :],
                                     ACT.Copy).then_inc(pre_a, 1)

            def emptied(n, dst, scale=1.0, cols=BANK, inc=True):
                act.wait_ge(pre_t, n + 1)
                src = pre_bank[n % 2][0:dst.shape[0], 0:cols]
                nc.scalar.activation(dst, src, ACT.Copy, scale=scale).then_inc(pre_a, 1)

            def flat(ap):
                return ap.rearrange("p a b -> p (a b)")

            def before_scores(s):
                if s == 1:
                    emptied(XN, flat(xnT[:, :, :]), cols=DM)
                if s == 2:
                    for n in range(4):
                        emptied(WK0 + n, flat(wkT[:, 4 * n:4 * n + 4, :]))
                if s == 7:
                    for h in range(H):
                        act.wait_ge(q_done, h // 4 + 1)
                        if h >= 4:
                            act.wait_ge(q_sq, h - 3)
                        nc.scalar.activation(junk_a[:, h % 4, :], q_bank[h // 4][:, D * (h % 4):D * (h % 4) + D],
                                             ACT.Square, accum_out=qsq[:, h:h + 1]).then_inc(q_sq, 1)
                if s == 10:
                    act.wait_ge(gg_ready, 1)
                    for n in range(4):
                        emptied(QT0 + n, flat(qT[:, 4 * n:4 * n + 4, :]), scale=gg_s[:, 0:1])
                if s == 12:
                    for n in range(4):
                        emptied(U0 + n, flat(u_hi[:, 4 * n:4 * n + 4, :]))
                if s == 14:
                    for n in range(4):
                        act.wait_ge(pre_t, WIN0 + n + 1)
                        for i in range(2):
                            src = pre_bank[(WIN0 + n) % 2][:, :].rearrange("p (j a e) -> p a j e", j=2, a=2)
                        nc.scalar.activation(
                            w_inT[:, :, 256 * n:256 * n + 256].rearrange("p a (j e) -> p a j e", j=2), src,
                            ACT.Copy).then_inc(pre_a, 1)
                    for n in range(2):
                        act.wait_ge(pre_t, WOUT0 + n + 1)
                        nc.scalar.activation(flat(w_outT[:, 2 * n:2 * n + 2, :]), pre_bank[(WOUT0 + n) % 2][:, :],
                                             ACT.Copy).then_inc(pre_a, 1)
                    act.wait_ge(pre_t, RW0 + 1)
                    nc.scalar.activation(rwT[:, :, :],
                                         pre_bank[RW0 % 2][:, 0:2 * P].rearrange("p (a e) -> p a e", a=2)[:, :, 0:E],
                                         ACT.Copy).then_inc(pre_a, 1)

            def exp_head(h):
                act.wait_ge(nmax_ready, h + 1)
                row = prob[(h // GH) % 2][:, h % GH, :]
                nc.scalar.activation(row, row, ACT.Exp, bias=nmax[:, h:h + 1],
                                     accum_out=psum_[:, h:h + 1]).then_inc(p_ready, 1)

            def leave_ctx(g):
                act.wait_ge(c_done, KT * (g + 1))
                if g == 0:
                    act.wait_ge(k_done, G * KT)
                if g > 0:
                    act.wait_ge(vo_done, g)
                nc.scalar.activation(oT[:, :], c_bank[:, :], ACT.Copy).then_inc(oT_ready, 1)

            def leave_value(g):
                act.wait_ge(voT_done, g + 1)
                if g > 0:
                    act.wait_ge(y_done, g)
                nc.scalar.activation(flat(voT[:, :, :]), v_bank[:, :], ACT.Copy).then_inc(voT_ready, 1)

            def norms_out(g):
                act.wait_ge(rk_turned, g + 1)
                if g > 0:
                    act.wait_ge(rrow_ld, 16 * GH * g)
                nc.scalar.activation(rkT[:, :], k_bank[0][0:GH * KT, 0:P], ACT.Copy).then_inc(rkT_ready, 1)

            for s in range(SLOTS):
                k, su, cu = s, s - S_AT, s - C_AT
                before_scores(s)
                for half in range(2):
                    if 0 <= cu < G * UNITS:
                        m = 2 * cu + half
                        act.wait_ge(t_done, m + 1)
                        if m >= 2:
                            act.wait_ge(c_done, m - 1)
                        nc.scalar.activation(pT_hi[:, m % 2, :], t_bank[m % 2][:, :], ACT.Copy).then_inc(hi_done, 1)
                        if m % KT == 0 and m > 0:
                            leave_ctx(m // KT - 1)
                if su > 0 and su % 2 == 0 and su <= G * UNITS:
                    exp_head(su // 2 - 1)
                if s % UNITS == R_TURN and 0 < s // UNITS <= G:
                    norms_out(s // UNITS - 1)
                if k < G * UNITS:
                    g, t = k // UNITS, 2 * (k % UNITS)
                    act.wait_ge(k_done, KT * g + t + 1)
                    for j in range(GH):
                        kj = k_bank[0][:, D * j:D * j + D]
                        last = nc.scalar.activation(kj, kj, ACT.Square, accum_out=ssq[:, g, j, t:t + 1])
                    last.then_inc(k_sq, 1)
                if cu >= UNITS and cu % UNITS == V_AT:
                    leave_value(cu // UNITS - 1)
                if s == G * UNITS + 10:
                    act.wait_ge(dt_neg, 1)
                    nc.scalar.activation(dt_sb[:, :], dt_sb[:, :], ACT.Exp, bias=dstat[:, 0:1], scale=-1.0,
                                         accum_out=dstat[:, 1:2]).then_inc(dt_exp, 1)
            leave_ctx(G - 1)
            leave_value(G - 1)

            act.wait_ge(clip_done, 1)
            for n in range(2):
                act.wait_ge(clip_done, n + 1)
                nc.scalar.activation(sg[:, n, :], zc[:, n, :], ACT.Sigmoid).then_inc(sig_done, 1)
            act.wait_ge(ooT_done, 1)
            nc.scalar.activation(flat(ooT[:, :, :]), bank[5][:, :], ACT.Copy).then_inc(ooT_ready, 1)
            act.wait_ge(t2, 2)
            nc.scalar.activation(flat(xmT[:, :, :]), bank[7][:, 0:DM], ACT.Copy).then_inc(a2, 1)
            act.wait_ge(lg_max, 1)
            nc.scalar.activation(ex[:, :], lg[:, :], ACT.Exp, bias=lstat[:, 1:2]).then_inc(lg_exp, 1)
            for e in range(E):
                act.wait_ge(gu_done, e + 1)
                if e >= 2:
                    act.wait_ge(act_ready, e - 1)
                nc.scalar.activation(silu_g[:, e % 2, :], bank[2 + e % 2][:, 0:I], ACT.Silu).then_inc(silu_done, 1)
                if e >= 1:
                    acts_turned(act, e - 1)
            acts_turned(act, E - 1)

        @block.vector
        def _(dve):
            steps = [0]

            def link(ins):
                steps[0] += 1
                ins.then_inc(dve_seq, 1)
                dve.wait_ge(dve_seq, steps[0])

            def rsqrt(y, v, t, done):
                link(nc.vector.tensor_scalar(out=y.bitcast(I32), in0=v.bitcast(I32), scalar1=1, scalar2=None,
                                             op0=ALU.logical_shift_right))
                link(nc.vector.tensor_scalar(out=y.bitcast(I32), in0=y.bitcast(I32), scalar1=-1.0,
                                             scalar2=float(0x5F3759DF), op0=ALU.mult, op1=ALU.add))
                for step in range(4):
                    link(nc.vector.scalar_tensor_tensor(out=t, in0=y, scalar=-0.5, in1=y, op0=ALU.mult, op1=ALU.mult))
                    link(nc.vector.tensor_tensor(out=t, in0=t, in1=v, op=ALU.mult))
                    last = nc.vector.scalar_tensor_tensor(out=y, in0=t, scalar=1.5, in1=y, op0=ALU.add, op1=ALU.mult)
                    if step < 3:
                        link(last)
                last.then_inc(done, 1)

            def ln_stats(n, src):
                link(nc.vector.bn_stats(out=stat[:, :], in_=src))
                link(nc.vector.bn_aggr(out=mv[:, :], in_=stat[:, :]))
                nc.vector.tensor_scalar(out=mv[:, 1:2], in0=mv[:, 1:2], scalar1=EPS, scalar2=None,
                                        op0=ALU.add).then_inc(var_ready, 1)
                dve.wait_ge(rstd_ready, n + 1)

            def normed(dst, src):
                return nc.vector.tensor_scalar(out=dst, in0=src, scalar1=mv[:, 0:1], scalar2=rstd[:, 0:1],
                                               op0=ALU.subtract, op1=ALU.mult)

            def flat(ap):
                return ap.rearrange("p a b -> p (a b)")

            for i in range(4):
                c0 = slice(i * BANK, i * BANK + BANK)
                dve.wait_ge(wk_hi_done, i + 1)
                nc.vector.tensor_tensor(out=wk_lo[:, c0], in0=wk_sb[:, c0], in1=wk_hi[:, c0].bitcast(F32),
                                        op=ALU.subtract).then_inc(wk_lo_done, 1)
                dve.wait_ge(pre_a, i + 1)
                nc.vector.tensor_tensor(out=ctxT_lo[:, c0], in0=pre_bank[i % 2][:, :],
                                        in1=ctxT_hi[:, c0].bitcast(F32), op=ALU.subtract).then_inc(pre_v, 1)
                if i == 1:
                    dve.wait_ge(ld_x, 16)
                    dve.wait_ge(mhalf_made, 1)
                    ln_stats(0, x_sb[:, :])
                    normed(xn[:, :], x_sb[:, :]).then_inc(ln_ready, 1)

            def before_scores(s):
                if s == 9:
                    dve.wait_ge(ld_g, 32)
                    nc.vector.scalar_tensor_tensor(out=gg_s[:, :], in0=gcol[:, 0:1], scalar=float(D) ** -0.5,
                                                   in1=gcol[:, 1:2], op0=ALU.mult, op1=ALU.mult).then_inc(gg_ready, 1)
                    dve.wait_ge(q_sq, H)
                    link(nc.vector.tensor_scalar(out=qsq[:, :], in0=qsq[:, :], scalar1=1.0 / D, scalar2=EPS,
                                                 op0=ALU.mult, op1=ALU.add))
                    rsqrt(rq[:, :], qsq[:, :], ta[:, 0:H], rq_ready)
                    dve.wait_ge(rq_ready, 1)
                    for n in range(4):
                        nc.vector.tensor_tensor(
                            out=q_sb[:, n * BANK:n * BANK + BANK].rearrange("p (h d) -> p h d", d=D),
                            in0=q_bank[n][:, :].rearrange("p (h d) -> p h d", d=D),
                            in1=rq[:, 4 * n:4 * n + 4].unsqueeze(2).to_broadcast([T, 4, D]),
                            op=ALU.mult).then_inc(q_norm, 1)
                if s == 12:
                    for n in range(4):
                        dve.wait_ge(pre_a, U0 + n + 1)
                        nc.vector.tensor_tensor(out=flat(u_lo[:, 4 * n:4 * n + 4, :]), in0=pre_bank[(U0 + n) % 2][:, :],
                                                in1=flat(u_hi[:, 4 * n:4 * n + 4, :]).bitcast(F32),
                                                op=ALU.subtract).then_inc(pre_v, 1)

            def k_stats(k):
                g, t = k // UNITS, 2 * (k % UNITS) + 1
                dve.wait_ge(k_done, KT * g + t + 1)
                for j in range(GH):
                    last = nc.vector.bn_stats(out=bn[:, j, t // 2, :], in_=k_bank[1][:, D * j:D * j + D])
                last.then_inc(k_bn, 1)

            def key_norms(g):
                odd = ssq[:, g, :, :].rearrange("p h (u two) -> p h u two", two=2)[:, :, :, 1]
                a = ta[:, 0:GH * UNITS].rearrange("p (h u) -> p h u", u=UNITS)
                b = tb[:, 0:GH * UNITS].rearrange("p (h u) -> p h u", u=UNITS)
                dve.wait_ge(k_bn, UNITS * (g + 1))
                link(nc.vector.tensor_tensor(out=a, in0=bn[:, :, :, 1], in1=bn[:, :, :, 1], op=ALU.mult))
                link(nc.vector.tensor_tensor(out=b, in0=bn[:, :, :, 4], in1=bn[:, :, :, 4], op=ALU.mult))
                link(nc.vector.tensor_tensor(out=a, in0=a, in1=b, op=ALU.add))
                link(nc.vector.scalar_tensor_tensor(out=a, in0=a, scalar=float(D // 2), in1=bn[:, :, :, 2],
                                                    op0=ALU.mult, op1=ALU.add))
                link(nc.vector.tensor_tensor(out=odd, in0=a, in1=bn[:, :, :, 5], op=ALU.add))
                dve.wait_ge(k_sq, UNITS * (g + 1))
                v = ssq[:, g, :, :].rearrange("p h t -> p (h t)")
                link(nc.vector.tensor_scalar(out=v, in0=v, scalar1=1.0 / D, scalar2=EPS, op0=ALU.mult, op1=ALU.add))
                rsqrt(rk[:, g, :, :].rearrange("p h t -> p (h t)"), v, ta[:, :], rk_ready)

            def scaled_scores(u, c2):
                h, c = u // 2, 2 * (u % 2) + c2
                n = NC * h + c
                g, j = h // GH, h % GH
                dve.wait_ge(s_done, n + 1)
                dve.wait_ge(rbc_ready, h + 1)
                if c == 0 and j == 0 and g >= 2:
                    dve.wait_ge(t_done, KT * (g - 1))
                c0 = slice(c * BANK, c * BANK + BANK)
                nc.vector.tensor_tensor_reduce(out=prob[g % 2][:, j, c0], in0=s_bank[n % 3][:, :],
                                               in1=rbc[h % 2][:, c0], scale=1.0, scalar=-3.0e38, op0=ALU.mult,
                                               op1=ALU.max, accum_out=smax[:, h, c:c + 1]).then_inc(sr_done, 1)
                if c == NC - 1:
                    dve.wait_ge(sr_done, n + 1)
                    link(nc.vector.tensor_reduce(out=pmax[:, h:h + 1], in_=smax[:, h, :], axis=AX.X, op=ALU.max))
                    nc.vector.tensor_scalar(out=nmax[:, h:h + 1], in0=pmax[:, h:h + 1], scalar1=-1.0, scalar2=None,
                                            op0=ALU.mult).then_inc(nmax_ready, 1)

            def scaled_value(g):
                h0 = GH * g
                dve.wait_ge(p_ready, h0 + GH)
                link(nc.vector.reciprocal(out=rs[:, h0:h0 + GH], in_=psum_[:, h0:h0 + GH]))
                dve.wait_ge(vo_done, g + 1)
                if g > 0:
                    dve.wait_ge(voT_done, g)
                nc.vector.tensor_tensor(out=vo_sb[:, :].rearrange("p (h d) -> p h d", d=D),
                                        in0=v_bank[:, :].rearrange("p (h d) -> p h d", d=D),
                                        in1=rs[:, h0:h0 + GH].unsqueeze(2).to_broadcast([T, GH, D]),
                                        op=ALU.mult).then_inc(vo_ready, 1)

            for s in range(SLOTS):
                k, su, cu = s, s - S_AT, s - C_AT
                before_scores(s)
                for half in range(2):
                    if 0 <= cu < G * UNITS:
                        m = 2 * cu + half
                        dve.wait_ge(hi_done, m + 1)
                        nc.vector.tensor_tensor(out=pT_lo[:, m % 2, :], in0=t_bank[m % 2][:, :],
                                                in1=pT_hi[:, m % 2, :].bitcast(F32), op=ALU.subtract).then_inc(lo_done, 1)
                    if 0 <= su < G * UNITS:
                        scaled_scores(su, half)
                if k < G * UNITS:
                    k_stats(k)
                    if k % UNITS == UNITS - 1:
                        key_norms(k // UNITS)
                if s == G * UNITS + 8:
                    dve.wait_ge(ld_dt, 16)
                    nc.vector.tensor_reduce(out=dstat[:, 0:1], in_=dt_sb[:, :], axis=AX.X,
                                            op=ALU.min).then_inc(dt_neg, 1)
                if s == G * UNITS + 12:
                    dve.wait_ge(dt_exp, 1)
                    link(nc.vector.reciprocal(out=dstat[:, 2:3], in_=dstat[:, 1:2]))
                    link(nc.vector.tensor_scalar(out=dt_sb[:, :], in0=dt_sb[:, :], scalar1=dstat[:, 2:3], scalar2=None,
                                                 op0=ALU.mult))
                if cu >= UNITS and cu % UNITS == V_AT:
                    scaled_value(cu // UNITS - 1)
            scaled_value(G - 1)

            dve.wait_ge(y_done, G)
            dve.wait_ge(c_done, G * KT)
            link(nc.vector.tensor_tensor(out=x1[:, :], in0=x_sb[:, :], in1=y_bank[:, 0:DM], op=ALU.add))
            ln_stats(1, x1[:, :])
            normed(y1[:, :], x1[:, :]).then_inc(ln_ready, 1)
            dve.wait_ge(ln_ready, 2)
            ln_stats(2, y1[:, :])
            normed(xn2[:, :], y1[:, :]).then_inc(ln_ready, 1)
            link(nc.vector.tensor_tensor(out=s1[:, :], in0=x1[:, :], in1=y1[:, :], op=ALU.add))
            dve.wait_ge(t2, 1)
            dve.wait_ge(ld_gb, 64)
            for a in range(DA):
                last = nc.vector.tensor_scalar(out=x2T[:, a, :], in0=bank[2][:, P * a:P * a + T],
                                               scalar1=gamma_c[:, a:a + 1], scalar2=beta_c[:, a:a + 1],
                                               op0=ALU.mult, op1=ALU.add)
            last.then_inc(a2, 1)
            for n in range(2):
                dve.wait_ge(pr_done, n + 1)
                nc.vector.tensor_scalar(out=zc[:, n, :], in0=bank[3 + n][:, :], scalar1=15.0, scalar2=-15.0,
                                        op0=ALU.min, op1=ALU.max).then_inc(clip_done, 1)
            dve.wait_ge(clip_done, 2)
            link(nc.vector.tensor_tensor(out=gg[:, :], in0=zc[:, 1, :], in1=dt_sb[:, :], op=ALU.mult))
            dve.wait_ge(sig_done, 1)
            link(nc.vector.tensor_tensor(out=zz[:, :], in0=bank[3][:, :], in1=sg[:, 0, :], op=ALU.mult))
            link(nc.vector.tensor_tensor(out=zz[:, :], in0=zz[:, :], in1=gg[:, :], op=ALU.mult))
            dve.wait_ge(sig_done, 2)
            nc.vector.tensor_tensor(out=oo[:, :], in0=zz[:, :], in1=sg[:, 1, :], op=ALU.mult).then_inc(oo_ready, 1)
            dve.wait_ge(mo_done, 1)
            link(nc.vector.tensor_tensor(out=x2[:, :], in0=bank[6][:, 0:DM], in1=s1[:, :], op=ALU.add))
            ln_stats(3, x2[:, :])
            normed(xm[:, :], x2[:, :]).then_inc(ln_ready, 1)

            dve.wait_ge(lg_done, 1)
            dve.wait_ge(ld_bias, 16)
            link(nc.vector.tensor_tensor(out=lg[:, :], in0=bank[0][:, 0:E], in1=bias_bc[:, :], op=ALU.add))
            link(nc.vector.tensor_reduce(out=lstat[:, 0:1], in_=lg[:, :], axis=AX.X, op=ALU.max))
            nc.vector.tensor_scalar(out=lstat[:, 1:2], in0=lstat[:, 0:1], scalar1=-1.0, scalar2=None,
                                    op0=ALU.mult).then_inc(lg_max, 1)
            dve.wait_ge(lg_exp, 1)
            dve.wait_ge(before_made, 2)
            other = ex[:, :].unsqueeze(1).to_broadcast([T, E, E])
            own = ex[:, :].unsqueeze(2).to_broadcast([T, E, E])
            link(nc.vector.tensor_tensor(out=cmp_a[:, :, :], in0=other, in1=own, op=ALU.is_equal))
            link(nc.vector.tensor_tensor(out=cmp_a[:, :, :], in0=cmp_a[:, :, :], in1=before[:, :, :], op=ALU.mult))
            link(nc.vector.tensor_tensor(out=cmp_b[:, :, :], in0=other, in1=own, op=ALU.is_gt))
            link(nc.vector.tensor_tensor(out=cmp_a[:, :, :], in0=cmp_a[:, :, :], in1=cmp_b[:, :, :], op=ALU.add))
            link(nc.vector.tensor_reduce(out=rank[:, :], in_=cmp_a[:, :, :], axis=AX.X, op=ALU.add))
            link(nc.vector.scalar_tensor_tensor(out=top[:, :], in0=rank[:, :], scalar=float(TOP_K), in1=ex[:, :],
                                                op0=ALU.is_lt, op1=ALU.mult))
            link(nc.vector.tensor_reduce(out=lstat[:, 2:3], in_=top[:, :], axis=AX.X, op=ALU.add))
            link(nc.vector.reciprocal(out=lstat[:, 3:4], in_=lstat[:, 2:3]))
            link(nc.vector.tensor_scalar(out=wgt[:, :], in0=top[:, :], scalar1=lstat[:, 3:4], scalar2=None, op0=ALU.mult))
            for e in range(E):
                dve.wait_ge(silu_done, e + 1)
                if e >= 2:
                    dve.wait_ge(at_done, e - 1)
                nc.vector.scalar_tensor_tensor(out=acts[:, e % 2, :], in0=silu_g[:, e % 2, :], scalar=wgt[:, e:e + 1],
                                               in1=bank[2 + e % 2][:, I:2 * I], op0=ALU.mult,
                                               op1=ALU.mult).then_inc(act_ready, 1)
            dve.wait_ge(dn_done, E)
            nc.vector.tensor_tensor(out=x3[:, :], in0=bank[7][:, 0:DM], in1=x2[:, :], op=ALU.add).then_inc(x3_ready, 1)


_INS = ['x', 'ctx_1024', 'L0_xattn_Wq', 'L0_xattn_Wk', 'L0_xattn_Wv', 'L0_xattn_Wo', 'L0_xattn_gq', 'L0_xattn_gk',
        'L0_attn_gamma', 'L0_attn_beta', 'L0_attn_W_in', 'L0_attn_W_out', 'L0_attn_dt', 'L0_ffn_router_w',
        'L0_ffn_expert_bias', 'L0_ffn_gate_proj', 'L0_ffn_up_proj', 'L0_ffn_down_proj']


def kernel(**inputs):
    import numpy as _np
    import concourse.bacc as _bacc
    from concourse import mybir as _mybir
    from concourse.bass_utils import run_bass_kernel_spmd as _run

    nc = _bacc.Bacc("TRN2", target_bir_lowering=False, num_devices=1)
    arrays, args = {}, []
    for name in _INS:
        a = _np.ascontiguousarray(inputs[name])
        arrays[f"in_{name}"] = a
        args.append(nc.dram_tensor(f"in_{name}", a.shape, _mybir.dt.from_np(a.dtype), kind="ExternalInput").ap())
    shape = inputs['x'].shape
    args.append(nc.dram_tensor("out_0", shape, _mybir.dt.float32, kind="ExternalOutput").ap())
    perceiver_layer(nc, *args)
    r = _run(nc, [arrays], core_ids=[0])
    return r.results[0]["out_0"]
```

```python
import concourse.bass as bass
from concourse import mybir

F32 = mybir.dt.float32
F32R = mybir.dt.float32r
I32 = mybir.dt.int32
ALU = mybir.AluOpType
ACT = mybir.ActivationFunctionType
AX = mybir.AxisListType

P = 128
EPS = 1e-5


def perceiver_layer(nc, x, ctx, Wq, Wk, Wv, Wo, gq, gk, gamma, beta, W_in, W_out, dt, router_w,
                    expert_bias, gate_proj, up_proj, down_proj, out):
    T, DM = x.shape[1], x.shape[2]
    NKEY, C = ctx.shape[1], ctx.shape[2]
    D = gq.shape[0]
    H = Wq.shape[1] // D
    KT = NKEY // P
    GH = 4
    G = H // GH
    BANK = 512
    NC = NKEY // BANK
    DI = dt.shape[0]
    E, I = gate_proj.shape[0], gate_proj.shape[2]
    IH = I // 2
    DA = DM // P
    TOP_K = 4
    PT = 3
    WS = 3
    GU = 4

    UNITS = KT // 2
    S_AT = 2 * UNITS
    C_AT = S_AT + UNITS + 1
    SLOTS = C_AT + G * UNITS
    N_AT = 1
    R_TURN = 3
    V_AT = 3
    EARLY = 2 * UNITS

    KB = 1024
    base = (nc.sbuf_base + 31) // 32 * 32

    def at(name, shape, kb, dtype=F32):
        return nc.alloc_sbuf_tensor_at(name, shape, dtype, offset=base + int(kb * KB))

    ctx_hi = at("ctx_hi", [P, KT, C], 0, F32R)
    ctx_lo = at("ctx_lo", [P, KT, C], 8, F32R)
    ctxT_hi = at("ctxT_hi", [C, NKEY], 16, F32R)
    ctxT_lo = at("ctxT_lo", [C, NKEY], 24, F32R)
    wk_hi = at("wk_hi", [C, H * D], 32, F32R)
    wk_lo = at("wk_lo", [C, H * D], 40, F32R)
    u_hi = at("u_hi", [C, H, T], 48, F32R)
    u_lo = at("u_lo", [C, H, T], 56, F32R)
    prob = [at(f"prob{i}", [T, GH, NKEY], 64 + 32 * i) for i in range(2)]
    rbc = [at(f"rbc{i}", [P, NKEY], 128 + 8 * i) for i in range(2)]
    rrow = at("rrow", [P, NKEY], 144)
    pT_hi = at("pT_hi", [P, PT, BANK], 152, F32R)
    pT_lo = at("pT_lo", [P, PT, BANK], 158, F32R)
    wv = at("wv", [C, H * D], 164)
    wo = at("wo", [D, H, DM], 172)
    w_inT = at("w_inT", [P, DA, 2 * DI], 188)
    w_outT = at("w_outT", [P, DI // P, DM], 196)
    small = [200.0]

    def tiny(name, shape, dtype=F32):
        n = 4
        for d in shape[1:]:
            n *= d
        t = at(name, shape, small[0], dtype)
        small[0] += (n + 31) // 32 * 32 / KB
        return t

    wq_sb = at("wq_sb", [P, DA, H * D], 64)
    q_sb = at("q_sb", [T, H * D], 80)
    qT = at("qT", [D, H, T], 88)
    wk_sb = at("wk_sb", [C, H * D], 96)
    wkT = at("wkT", [D, H, C], 104)
    w_in_sb = at("w_in_sb", [P, 2 * DI // P, DM], 112)
    w_out_sb = at("w_out_sb", [P, DA, DI], 120)
    junk_a = at("junk_a", [P, 4, D], 124)
    xn = at("xn", [T, DM], 126)
    xnT = at("xnT", [P, DA, T], 127)
    rw_sb = at("rw_sb", [E, DM], 152)
    ctx_sb = at("ctx_sb", [P, KT, C], 128)
    oT = at("oT", [C, GH * T], 32)
    vo_sb = at("vo_sb", [T, GH * D], 34)
    voT = at("voT", [D, GH, T], 36)
    dt_sb = at("dt_sb", [P, DI], 38)
    guw = at("guw", [P, E, DA, 2 * I], 64)
    dww = at("dww", [IH, E, 2, DM], 120)
    x1 = at("x1", [T, DM], 0)
    y1 = at("y1", [T, DM], 1)
    s1 = at("s1", [T, DM], 2)
    xn2 = at("xn2", [T, DM], 3)
    x2 = at("x2", [T, DM], 4)
    xm = at("xm", [T, DM], 5)
    x2T = at("x2T", [P, DA, T], 6)
    xmT = at("xmT", [P, DA, T], 7)
    zc = at("zc", [T, 2, DI], 8)
    sg = at("sg", [T, 2, DI], 12)
    zz = at("zz", [T, DI], 16)
    gg = at("gg", [T, DI], 18)
    oo = at("oo", [T, DI], 20)
    ooT = at("ooT", [P, DI // P, T], 22)
    silu_g = at("silu_g", [T, 2, I], 24)
    acts = at("acts", [T, 2, I], 26)
    xmT_hi = at("xmT_hi", [P, DA, T], 43, F32R)
    xmT_lo = at("xmT_lo", [P, DA, T], 44, F32R)
    actT_hi = at("actT_hi", [IH, 2, 2, T], 45, F32R)
    actT_lo = at("actT_lo", [IH, 2, 2, T], 47, F32R)
    gu_hi = at("gu_hi", [P, WS, DA, 2 * I], 152, F32R)
    gu_lo = at("gu_lo", [P, WS, DA, 2 * I], 162.5, F32R)
    dw_hi = at("dw_hi", [IH, WS, 2, DM], 173, F32R)
    dw_lo = at("dw_lo", [IH, WS, 2, DM], 179, F32R)
    x3 = at("x3", [T, DM], 30)

    ident = tiny("ident", [P, P])
    x_sb = tiny("x_sb", [T, DM])
    ssq = tiny("ssq", [P, G, GH, KT])
    bn = tiny("bn", [P, 2, GH, UNITS, 6])
    rk = tiny("rk", [P, G, GH, KT])
    ta = tiny("ta", [P, GH * KT])
    tb = tiny("tb", [P, GH * KT])
    rkT = tiny("rkT", [GH * KT, P])
    qsq = tiny("qsq", [T, H])
    rq = tiny("rq", [T, H])
    gcol = tiny("gcol", [D, 2])
    gg_s = tiny("gg_s", [D, 1])
    gamma_c = tiny("gamma_c", [P, DA])
    beta_c = tiny("beta_c", [P, DA])
    stat = tiny("stat", [T, 6])
    mv = tiny("mv", [T, 2])
    rstd = tiny("rstd", [T, 1])
    mhalf = tiny("mhalf", [P, 1])
    smax = tiny("smax", [T, H, NC])
    nmax = tiny("nmax", [T, H])
    pmax = tiny("pmax", [T, H])
    psum_ = tiny("psum_", [T, H])
    rs = tiny("rs", [T, H])
    rwT = tiny("rwT", [P, DA, E])
    bias_bc = tiny("bias_bc", [P, E])
    dstat = tiny("dstat", [P, 4])
    lg = tiny("lg", [T, E])
    ex = tiny("ex", [T, E])
    rank = tiny("rank", [T, E])
    top = tiny("top", [T, E])
    wgt = tiny("wgt", [T, E])
    lstat = tiny("lstat", [T, 4])
    cmp_a = at("cmp_a", [T, E, E], 41)
    cmp_b = at("cmp_b", [T, E, E], 42)
    before = at("before", [P, E, E], 40)
    assert base + small[0] * KB <= nc.sbuf_usable_end, small[0]

    bank = [nc.alloc_psum_tensor(f"bank{i}", [P, BANK], F32) for i in range(8)]
    k_bank = bank[0:4]
    s_bank = bank[2:5]
    t_bank = bank[5:7]
    c_bank = bank[7]
    q_bank = [bank[4], bank[5]]
    pre_bank = [bank[6], bank[7]]
    v_bank, y_bank = bank[0:2]

    x_bank, g_bank, z_bank, o_bank = (bank[2], bank[5]), bank[3], (bank[4], bank[0]), bank[6]
    gu_bank, a_bank, d_bank, l_bank = bank[1:1 + GU], bank[5:7], bank[7], bank[0]

    def k_home(n):
        return k_bank[n % 4 if n < 2 * EARLY else n % 2]

    def norm_bank(g):
        return k_home(min(KT * (g + 1) + 2 * R_TURN, KT * G))

    def k_before(n):
        return n // 2 - 1 if n < 2 * EARLY + 2 else n // 2

    EXPERTS = ((0, 4), (4, 9), (9, E))
    FIRST_OF = {lo: n for n, (lo, hi) in enumerate(EXPERTS)}

    def sem(name):
        return nc.alloc_semaphore(name)

    ld_x, ld_wq, ld_g, ld_win, ld_wout, ld_gb = map(sem, (
        "ld_x", "ld_wq", "ld_g", "ld_win", "ld_wout", "ld_gb"))
    ld_rw, ld_bias, ld_wv, ld_wo, ld_dt = map(sem, ("ld_rw", "ld_bias", "ld_wv", "ld_wo", "ld_dt"))
    ld_ctx = [sem(f"ld_ctx{i}") for i in range(2)]
    ld_wk = [sem(f"ld_wk{i}") for i in range(2)]
    ld_exp = [sem(f"ld_exp{i}") for i in range(4)]
    ident_made, mhalf_made, before_made = map(sem, ("ident_made", "mhalf_made", "before_made"))
    ctx_hi_done, ctx_lo_done = map(sem, ("ctx_hi_done", "ctx_lo_done"))
    pre_t, pre_a, pre_v = map(sem, ("pre_t", "pre_a", "pre_v"))
    wk_hi_done, wk_lo_done = map(sem, ("wk_hi_done", "wk_lo_done"))
    k_done, k_sq, k_bn, rk_ready, rk_turned, rkT_ready, rrow_ld, rbc_ready = map(sem, (
        "k_done", "k_sq", "k_bn", "rk_ready", "rk_turned", "rkT_ready", "rrow_ld", "rbc_ready"))
    var_ready, rstd_ready, ln_ready = map(sem, ("var_ready", "rstd_ready", "ln_ready"))
    q_done, q_sq, q_norm, u_done = map(sem, ("q_done", "q_sq", "q_norm", "u_done"))
    s_done, sr_done, nmax_ready, p_ready = map(sem, ("s_done", "sr_done", "nmax_ready", "p_ready"))
    t_done, hi_done, lo_done, c_done, oT_ready = map(sem, (
        "t_done", "hi_done", "lo_done", "c_done", "oT_ready"))
    vo_done, vo_ready, voT_done, voT_ready, y_done = map(sem, (
        "vo_done", "vo_ready", "voT_done", "voT_ready", "y_done"))
    a2_a, a2_v, s1_ready, xh_ready, xl_ready, gh_ready, gl_ready, ah_ready, al_ready, dh_ready, dl_ready = map(sem, (
        "a2_a", "a2_v", "s1_ready", "xh_ready", "xl_ready", "gh_ready", "gl_ready", "ah_ready", "al_ready",
        "dh_ready", "dl_ready"))
    t2, pr_done, clip_done, sig_done, oo_ready, ooT_done, ooT_ready, mo_done = map(sem, (
        "t2", "pr_done", "clip_done", "sig_done", "oo_ready", "ooT_done", "ooT_ready", "mo_done"))
    dt_neg, dt_exp, lg_done, lg_max, lg_exp = map(sem, ("dt_neg", "dt_exp", "lg_done", "lg_max", "lg_exp"))
    gu_done, silu_done, act_ready, at_done, dn_done, x3_ready, stored = map(sem, (
        "gu_done", "silu_done", "act_ready", "at_done", "dn_done", "x3_ready", "stored"))
    dve_seq, gg_ready, rq_ready = map(sem, ("dve_seq", "gg_ready", "rq_ready"))
    pool_seq, pool_sq, kv_ready, q_copied = map(sem, ("pool_seq", "pool_sq", "kv_ready", "q_copied"))

    CTX0, XN, WK0, QT0, U0, WIN0, WOUT0, RW0 = 0, 4, 5, 9, 13, 17, 21, 23
    EMPTIER = ["av"] * 4 + ["a"] + ["v"] * 4 + ["a"] * 4 + ["av"] * 4 + ["v"] * 4 + ["a"] * 2 + ["a"]

    def by(n, who):
        return sum(who in e for e in EMPTIER[:n + 1])

    block = nc.Block()
    with block:
        def load_experts(eng, lo, hi, done):
            gv = gate_proj.rearrange("e (a p) i -> p e a i", p=P)
            uv = up_proj.rearrange("e (a p) i -> p e a i", p=P)
            for a in range(DA):
                eng.dma_start(guw[:, lo:hi, a, 0:I], gv[:, lo:hi, a, :]).then_inc(done, 16)
                eng.dma_start(guw[:, lo:hi, a, I:2 * I], uv[:, lo:hi, a, :]).then_inc(done, 16)

        CTX_V = 4

        def rstd_of(pool, n):
            pool.wait_ge(var_ready, n + 1)
            pool.tensor_tensor(out=rstd[:, :], in0=mv[:, 1:2], in1=mhalf[0:T, :], op=ALU.pow).then_inc(rstd_ready, 1)

        @block.sync
        def _(sp):
            ctx_v = ctx[0, :, :].rearrange("(p t) c -> p t c", t=KT)
            for i in range(2):
                sp.dma_start(ctx_sb[:, 8 * i:8 * i + 8, :], ctx_v[:, 8 * i:8 * i + 8, :]).then_inc(ld_ctx[i], 16)
            sp.dma_start(wq_sb[:, :, :], Wq.rearrange("(a p) n -> p a n", p=P)).then_inc(ld_wq, 16)
            sp.dma_start(gcol[:, 0:1], gq.rearrange("(p a) -> p a", a=1)).then_inc(ld_g, 16)
            sp.dma_start(gcol[:, 1:2], gk.rearrange("(p a) -> p a", a=1)).then_inc(ld_g, 16)
            sp.dma_start(w_in_sb[:, :, :], W_in.rearrange("(j p) d -> p j d", p=P)).then_inc(ld_win, 16)
            sp.dma_start(w_out_sb[:, :, :], W_out.rearrange("(a p) e -> p a e", p=P)).then_inc(ld_wout, 16)
            sp.dma_start(rw_sb[:, :], router_w).then_inc(ld_rw, 16)
            sp.dma_start(wv[:, :], Wv).then_inc(ld_wv, 16)
            sp.dma_start(wo[:, :, :], Wo.rearrange("(h d) n -> d h n", d=D)).then_inc(ld_wo, 16)
            for a in range(DA):
                for dst, src in ((gamma_c, gamma), (beta_c, beta)):
                    sp.dma_start(dst[:, a:a + 1], src[P * a:P * a + P].rearrange("(p o) -> p o", o=1)).then_inc(ld_gb, 16)
            sp.dma_start(bias_bc[:, :], expert_bias.rearrange("(a e) -> a e", a=1).to_broadcast([P, E])).then_inc(ld_bias, 16)
            for g in range(G):
                sp.wait_ge(rkT_ready, g + 1)
                if g > 0:
                    sp.wait_ge(rbc_ready, GH * g)
                for j in range(GH):
                    sp.dma_start(rrow[32 * j:32 * j + 1, :].rearrange("a (t p) -> a t p", p=P),
                                 rkT[KT * j:KT * j + KT, :]).then_inc(rrow_ld, 16)
            sp.wait_ge(k_done, G * KT)
            sp.dma_start(dt_sb[:, :], dt.rearrange("(a e) -> a e", a=1).to_broadcast([P, DI])).then_inc(ld_dt, 16)
            sp.wait_ge(t_done, 3 * KT)
            for n, (lo, hi) in enumerate(EXPERTS[:2]):
                load_experts(sp, lo, hi, ld_exp[n])
            sp.wait_ge(t_done, 4 * KT)
            sp.wait_ge(sr_done, H * NC)
            load_experts(sp, *EXPERTS[2], ld_exp[2])
            down_v = down_proj.rearrange("e (a p) d -> p e a d", p=IH)
            for a in range(2):
                sp.dma_start(dww[:, :, a, :], down_v[:, :, a, :]).then_inc(ld_exp[3], 16)
            sp.wait_ge(x3_ready, 1)
            sp.dma_start(out[0, :, :], x3[:, :]).then_inc(stored, 16)
            sp.wait_ge(stored, 16)

        def mean_squares(pool, g):
            odd = ssq[:, g, :, :].rearrange("p h (u two) -> p h u two", two=2)[:, :, :, 1]
            steps = [4 * g]

            def link(ins):
                steps[0] += 1
                ins.then_inc(pool_seq, 1)
                pool.wait_ge(pool_seq, steps[0])

            pool.wait_ge(k_bn, UNITS * (g + 1))
            sq_mean = tb[:, :].rearrange("p (h u two) -> p h u two", h=GH, two=2)
            half = bn[:, g % 2, :, :, :].rearrange("p h u (two f) -> p h u two f", two=2)
            for i in range(2):
                mean_i, m2_i, s_i = half[:, :, :, i, 1], half[:, :, :, i, 2], sq_mean[:, :, :, i]
                nc.gpsimd.tensor_tensor(out=s_i, in0=mean_i, in1=mean_i, op=ALU.mult).then_inc(pool_sq, 1)
            pool.wait_ge(pool_sq, 2 * (g + 1))
            link(nc.gpsimd.tensor_tensor(out=odd, in0=sq_mean[:, :, :, 0], in1=sq_mean[:, :, :, 1], op=ALU.add))
            link(nc.gpsimd.tensor_scalar(out=odd, in0=odd, scalar1=float(D // 2), scalar2=0.0, op0=ALU.mult, op1=ALU.add))
            link(nc.gpsimd.tensor_tensor(out=odd, in0=odd, in1=half[:, :, :, 0, 2], op=ALU.add))
            link(nc.gpsimd.tensor_tensor(out=odd, in0=odd, in1=half[:, :, :, 1, 2], op=ALU.add))
            pool.wait_ge(k_sq, UNITS * (g + 1))
            v = ssq[:, g, :, :].rearrange("p h t -> p (h t)")
            nc.gpsimd.tensor_scalar(out=v, in0=v, scalar1=1.0 / D, scalar2=EPS, op0=ALU.mult,
                                    op1=ALU.add).then_inc(kv_ready, 1)

        @block.gpsimd
        def _(pool):
            pool.memset(ident[:, :], 0.0).then_inc(ident_made, 1)
            pool.wait_ge(ident_made, 1)
            pool.affine_select(out=ident[:, :], in_=ident[:, :], compare_op=ALU.not_equal, fill=1.0, base=0,
                               pattern=[[-1, P]], channel_multiplier=1).then_inc(ident_made, 1)
            pool.memset(mhalf[:, :], -0.5).then_inc(mhalf_made, 1)
            for i in range(4):
                pool.wait_ge(ld_ctx[i // 2], 16)
                t0, t1 = 4 * i, 4 * i + 4
                pool.tensor_scalar(out=ctx_hi[:, t0:t1, :], in0=ctx_sb[:, t0:t1, :], scalar1=1.0, scalar2=0.0,
                                   op0=ALU.mult, op1=ALU.add).then_inc(ctx_hi_done, 1)
                pool.wait_ge(ctx_hi_done, i + 1)
                pool.tensor_tensor(out=ctx_lo[:, t0:t1, :], in0=ctx_sb[:, t0:t1, :],
                                   in1=ctx_hi[:, t0:t1, :].bitcast(F32), op=ALU.subtract).then_inc(ctx_lo_done, 1)
                if i == 1:
                    rstd_of(pool, 0)
            mean_squares(pool, 0)
            pool.wait_ge(kv_ready, 1)
            for h in range(H):
                g, j = h // GH, h % GH
                pool.wait_ge(rrow_ld, 16 * GH * (g + 1))
                if h >= 2:
                    pool.wait_ge(sr_done, NC * (h - 1))
                if h < 2:
                    pool.wait_ge(pre_v, CTX_V)
                    pool.wait_ge(ctx_lo_done, 4)
                pool.partition_broadcast(rbc[h % 2][:, :], rrow[32 * j:32 * j + 1, :]).then_inc(rbc_ready, 1)
                if j == 1 and g + 1 < G:
                    pool.wait_ge(rbc_ready, h + 1)
                    mean_squares(pool, g + 1)
                    pool.wait_ge(kv_ready, g + 2)
            pool.wait_ge(k_done, G * KT)
            pool.memset(before[:, :, :], 1.0).then_inc(before_made, 1)
            pool.wait_ge(before_made, 1)
            pool.affine_select(out=before[:, :, :], in_=before[:, :, :], compare_op=ALU.is_gt, fill=0.0, base=0,
                               pattern=[[1, E], [-1, E]], channel_multiplier=0).then_inc(before_made, 1)
            rstd_of(pool, 1)
            rstd_of(pool, 2)
            pool.wait_ge(y_done, G)
            pool.wait_ge(ld_exp[3], 32)
            for e in range(E):
                if e >= WS:
                    pool.wait_ge(dn_done, e - WS + 1)
                src, hi, lo = (w[:, i, :, :].rearrange("p a d -> p (a d)") for w, i in (
                    (dww, e), (dw_hi, e % WS), (dw_lo, e % WS)))
                pool.tensor_scalar(out=hi, in0=src, scalar1=1.0, scalar2=0.0, op0=ALU.mult,
                                   op1=ALU.add).then_inc(dh_ready, 1)
                pool.wait_ge(dh_ready, e + 1)
                pool.tensor_tensor(out=lo, in0=src, in1=hi.bitcast(F32), op=ALU.subtract).then_inc(dl_ready, 1)
                if e == 1:
                    rstd_of(pool, 3)

        @block.tensor
        def _(pe):
            def turn(n, pieces, need=None):
                if n >= 2 and "a" in EMPTIER[n - 2]:
                    pe.wait_ge(pre_a, by(n - 2, "a"))
                if n >= 2 and "v" in EMPTIER[n - 2]:
                    pe.wait_ge(pre_v, by(n - 2, "v"))
                for i, emit in enumerate(pieces):
                    last = emit(pre_bank[n % 2], i)
                last.then_inc(pre_t, 1)

            def turned(src, rows=P):
                cols = src.shape[1]
                return lambda b, i: nc.tensor.transpose(b[0:cols, P * i:P * i + rows], src, ident[0:rows, 0:rows])

            pe.wait_ge(ident_made, 2)
            for n in range(4):
                pe.wait_ge(ld_ctx[n // 2], 16)
                turn(CTX0 + n, [turned(ctx_sb[:, 4 * n + i, :]) for i in range(4)])

            def three_passes(dst, w_hi, w_lo, m_hi, m_lo):
                nc.tensor.matmul(dst, w_hi, m_hi, start=True, stop=False)
                nc.tensor.matmul(dst, w_hi, m_lo, start=False, stop=False)
                return nc.tensor.matmul(dst, w_lo, m_hi, start=False, stop=True)

            def k_unit(s):
                g = s // UNITS
                if s % UNITS == R_TURN and g > 0:
                    turn_norms(g - 1)
                for t in (2 * (s % UNITS), 2 * (s % UNITS) + 1):
                    n = KT * g + t
                    if k_before(n) > 0:
                        pe.wait_ge((k_sq, k_bn)[t % 2], k_before(n))
                    if g > 0 and t == 2 * R_TURN:
                        pe.wait_ge(rkT_ready, g)
                    if t == 0:
                        pe.wait_ge(wk_lo_done, g + 1)
                        pe.wait_ge(wk_hi_done, g + 1)
                    if g == 0 and t % 4 == 0:
                        pe.wait_ge(pre_v, t // 4 + 1)
                        pe.wait_ge(pre_a, t // 4 + 1)
                    c0 = slice(t * P, t * P + P)
                    w0 = slice(g * BANK, g * BANK + BANK)
                    three_passes(k_home(n)[:, :], ctxT_hi[:, c0], ctxT_lo[:, c0],
                                 wk_hi[:, w0], wk_lo[:, w0]).then_inc(k_done, 1)

            def turn_norms(g):
                pe.wait_ge(rk_ready, g + 1)
                pe.wait_ge(k_sq, min(UNITS * (g + 1) + R_TURN, UNITS * G))
                nc.tensor.transpose(norm_bank(g)[0:GH * KT, 0:P], rk[:, g, :, :].rearrange("p h t -> p (h t)"),
                                    ident[:, :]).then_inc(rk_turned, 1)

            def q_products(n):
                if n == 0:
                    pe.wait_ge(ld_wq, 16)
                    pe.wait_ge(pre_a, by(XN, "a"))
                if n >= 2:
                    pe.wait_ge(q_sq, GH * (n - 1))
                for a in range(DA):
                    last = nc.tensor.matmul(q_bank[n % 2][:, :], xnT[:, a, :], wq_sb[:, a, n * BANK:n * BANK + BANK],
                                            start=(a == 0), stop=(a == DA - 1))
                last.then_inc(q_done, 1)

            def before_scores(s):
                if s == 1:
                    pe.wait_ge(ln_ready, 1)
                    turn(XN, [turned(xn[:, P * a:P * a + P]) for a in range(DA)])
                if s in (2, 3):
                    if s == 2:
                        pe.wait_ge(ld_wk[1], 16)
                    for n in (2 * s - 4, 2 * s - 3):
                        turn(WK0 + n, [turned(wk_sb[:, P * h:P * h + P]) for h in range(4 * n, 4 * n + 4)])
                if 4 <= s < 8:
                    q_products(s - 4)
                if s in (9, 10):
                    for n in (2 * s - 18, 2 * s - 17):
                        pe.wait_ge(q_norm, n + 1)
                        turn(QT0 + n, [turned(q_sb[:, P * h:P * h + P]) for h in range(4 * n, 4 * n + 4)])
                if s in (11, 12):
                    if s == 11:
                        pe.wait_ge(pre_a, by(QT0 + 3, "a"))
                        pe.wait_ge(pre_v, by(WK0 + 3, "v"))
                    for n in (2 * s - 22, 2 * s - 21):
                        turn(U0 + n, [
                            lambda b, i, h=h: nc.tensor.matmul(b[:, P * i:P * i + T], wkT[:, h, :], qT[:, h, :],
                                                               start=True, stop=True)
                            for h in range(4 * n, 4 * n + 4)])
                if s in (13, 14):
                    if s == 13:
                        pe.wait_ge(ld_win, 16)
                    for n in (2 * s - 26, 2 * s - 25):
                        turn(WIN0 + n, [turned(w_in_sb[:, 2 * n + i // 2, P * (i % 2):P * (i % 2) + P])
                                        for i in range(4)])
                if s == 15:
                    pe.wait_ge(ld_wout, 16)
                    for n in range(2):
                        turn(WOUT0 + n, [turned(w_out_sb[:, i % 2, P * (2 * n + i // 2):P * (2 * n + i // 2) + P])
                                         for i in range(4)])
                    pe.wait_ge(ld_rw, 16)
                    turn(RW0, [turned(rw_sb[:, P * a:P * a + P], rows=E) for a in range(DA)])

            def s_chunk(u, c2):
                h, c = u // 2, 2 * (u % 2) + c2
                n = NC * h + c
                if n == 0:
                    pe.wait_ge(pre_a, by(RW0, "a"))
                    pe.wait_ge(pre_v, by(RW0, "v"))
                    pe.wait_ge(q_sq, H)
                if n < 3:
                    pe.wait_ge(k_sq, EARLY)
                    pe.wait_ge(k_bn, EARLY)
                if n >= 3:
                    pe.wait_ge(sr_done, n - 2)
                c0 = slice(c * BANK, c * BANK + BANK)
                three_passes(s_bank[n % 3][:, :], u_hi[:, h, :], u_lo[:, h, :],
                             ctxT_hi[:, c0], ctxT_lo[:, c0]).then_inc(s_done, 1)

            def turn_probs(m):
                g, kt = m // KT, m % KT
                if kt == 0:
                    pe.wait_ge(p_ready, GH * (g + 1))
                if m >= 2:
                    pe.wait_ge(lo_done, m - 1)
                for j in range(GH):
                    last = nc.tensor.transpose(t_bank[m % 2][:, P * j:P * j + T],
                                               prob[g % 2][:, j, kt * P:kt * P + P], ident[:, :])
                last.then_inc(t_done, 1)

            def times_ctx(m):
                g, kt = m // KT, m % KT
                if kt == 0 and g > 0:
                    pe.wait_ge(oT_ready, g)
                if m == 0:
                    pe.wait_ge(ctx_lo_done, 4)
                pe.wait_ge(lo_done, m + 1)
                pe.wait_ge(hi_done, m + 1)
                hi, lo = pT_hi[:, m % PT, :], pT_lo[:, m % PT, :]
                nc.tensor.matmul(c_bank[:, :], ctx_hi[:, kt, :], hi, start=(kt == 0), stop=False)
                nc.tensor.matmul(c_bank[:, :], ctx_lo[:, kt, :], hi, start=False, stop=False)
                nc.tensor.matmul(c_bank[:, :], ctx_hi[:, kt, :], lo, start=False,
                                 stop=(kt == KT - 1)).then_inc(c_done, 1)

            def values(g):
                pe.wait_ge(oT_ready, g + 1)
                if g == 0:
                    pe.wait_ge(ld_wv, 16)
                    pe.wait_ge(ld_wo, 16)
                    pe.wait_ge(k_sq, UNITS * G)
                    pe.wait_ge(k_bn, UNITS * G)
                    pe.wait_ge(rkT_ready, G)
                if g > 0:
                    pe.wait_ge(voT_ready, g)
                for j in range(GH):
                    h = GH * g + j
                    last = nc.tensor.matmul(v_bank[:, D * j:D * j + D], oT[:, T * j:T * j + T], wv[:, D * h:D * h + D],
                                            start=True, stop=True)
                last.then_inc(vo_done, 1)

            def turn_values(g):
                pe.wait_ge(vo_ready, g + 1)
                for j in range(GH):
                    last = nc.tensor.transpose(v_bank[:, T * j:T * j + T], vo_sb[:, D * j:D * j + D], ident[:, :])
                last.then_inc(voT_done, 1)

            def into_out(g):
                pe.wait_ge(voT_ready, g + 1)
                for j in range(GH):
                    h = GH * g + j
                    last = nc.tensor.matmul(y_bank[:, 0:DM], voT[:, j, :], wo[:, h, :],
                                            start=(h == 0), stop=(h == H - 1))
                last.then_inc(y_done, 1)

            for s in range(SLOTS):
                k, su, cu = s, s - S_AT, s - C_AT
                before_scores(s)
                for half in range(2):
                    if 0 <= cu < G * UNITS:
                        m = 2 * cu + half
                        turn_probs(m)
                        if m >= 2:
                            times_ctx(m - 2)
                    if 0 <= su < G * UNITS:
                        s_chunk(su, half)
                if k < G * UNITS:
                    k_unit(k)
                if s == G * UNITS + R_TURN:
                    turn_norms(G - 1)
                if cu >= UNITS:
                    if cu % UNITS == V_AT:
                        values(cu // UNITS - 1)
                    if cu % UNITS == V_AT + 1:
                        turn_values(cu // UNITS - 1)
                    if cu % UNITS == V_AT + 2:
                        into_out(cu // UNITS - 1)
            times_ctx(G * KT - 2)
            times_ctx(G * KT - 1)
            values(G - 1)
            turn_values(G - 1)
            into_out(G - 1)

            pe.wait_ge(ln_ready, 3)
            for a in range(DA):
                nc.tensor.transpose(x_bank[a][:, 0:T], xn2[:, P * a:P * a + P], ident[:, :]).then_inc(t2, 1)
            pe.wait_ge(a2_v, 1)
            pe.wait_ge(a2_a, 1)
            for dst, w0, w in ((g_bank, DI, DI), (z_bank[0], 0, DI // 2), (z_bank[1], DI // 2, DI // 2)):
                for a in range(DA):
                    last = nc.tensor.matmul(dst[:, 0:w], x2T[:, a, :], w_inT[:, a, w0:w0 + w],
                                            start=(a == 0), stop=(a == DA - 1))
                last.then_inc(pr_done, 1)
            for i in range(2):
                pe.wait_ge(oo_ready, i + 1)
                for n in range(2):
                    last = nc.tensor.transpose(x_bank[i][:, P * n:P * n + T], oo[:, P * (2 * i + n):P * (2 * i + n) + P],
                                               ident[:, :])
                last.then_inc(ooT_done, 1)
            for i in range(2):
                pe.wait_ge(ooT_ready, i + 1)
                for n in (2 * i, 2 * i + 1):
                    last = nc.tensor.matmul(o_bank[:, 0:DM], ooT[:, n, :], w_outT[:, n, :],
                                            start=(n == 0), stop=(n == DI // P - 1))
            last.then_inc(mo_done, 1)

            pe.wait_ge(ln_ready, 4)
            for a in range(DA):
                last = nc.tensor.transpose(d_bank[:, P * a:P * a + T], xm[:, P * a:P * a + P], ident[:, :])
            last.then_inc(t2, 1)
            pe.wait_ge(a2_a, 2)
            for a in range(DA):
                last = nc.tensor.matmul(l_bank[:, 0:E], xmT[:, a, :], rwT[:, a, :], start=(a == 0), stop=(a == DA - 1))
            last.then_inc(lg_done, 1)

            def halves_product(dst, w, m, first, last):
                (w_hi, w_lo), (m_hi, m_lo) = w, m
                nc.tensor.matmul(dst, w_hi, m_hi, start=first, stop=False)
                nc.tensor.matmul(dst, w_hi, m_lo, start=False, stop=False)
                return nc.tensor.matmul(dst, w_lo, m_hi, start=False, stop=last)

            def gate_up(e):
                if e == 0:
                    pe.wait_ge(xl_ready, 1)
                pe.wait_ge(gl_ready, e + 1)
                if e >= GU:
                    pe.wait_ge(act_ready, e - GU + 1)
                for a in range(DA):
                    last = halves_product(gu_bank[e % GU][:, 0:2 * I], (xmT_hi[:, a, :], xmT_lo[:, a, :]),
                                          (gu_hi[:, e % WS, a, :], gu_lo[:, e % WS, a, :]), a == 0, a == DA - 1)
                last.then_inc(gu_done, 1)

            def turn_acts(e):
                pe.wait_ge(act_ready, e + 1)
                if e >= 2:
                    pe.wait_ge(al_ready, e - 1)
                for a in range(2):
                    last = nc.tensor.transpose(a_bank[e % 2][0:IH, T * a:T * a + T], acts[:, e % 2, IH * a:IH * a + IH],
                                               ident[:, :])
                last.then_inc(at_done, 1)

            def down(e):
                pe.wait_ge(al_ready, e + 1)
                pe.wait_ge(dl_ready, e + 1)
                for a in range(2):
                    last = halves_product(d_bank[:, 0:DM], (actT_hi[:, e % 2, a, :], actT_lo[:, e % 2, a, :]),
                                          (dw_hi[:, e % WS, a, :], dw_lo[:, e % WS, a, :]),
                                          e == 0 and a == 0, e == E - 1 and a == 1)
                last.then_inc(dn_done, 1)

            for e in range(E + 2):
                if e < E:
                    gate_up(e)
                if 1 <= e <= E:
                    turn_acts(e - 1)
                if e >= 2:
                    down(e - 2)

        @block.scalar
        def _(act):
            act.dma_start(wk_sb[:, 0:BANK], Wk[:, 0:BANK]).then_inc(ld_wk[0], 16)
            act.dma_start(x_sb[:, :], x[0, :, :]).then_inc(ld_x, 16)
            act.dma_start(wk_sb[:, BANK:], Wk[:, BANK:]).then_inc(ld_wk[1], 16)

            def wk_half(i):
                act.wait_ge(ld_wk[min(i, 1)], 16)
                nc.scalar.activation(wk_hi[:, i * BANK:i * BANK + BANK], wk_sb[:, i * BANK:i * BANK + BANK],
                                     ACT.Copy).then_inc(wk_hi_done, 1)

            for i in range(4):
                if i == 1:
                    wk_half(0)
                act.wait_ge(pre_t, i + 1)
                nc.scalar.activation(ctxT_hi[:, i * BANK:i * BANK + BANK], pre_bank[i % 2][:, :],
                                     ACT.Copy).then_inc(pre_a, 1)

            def emptied(n, dst, scale=1.0, cols=BANK, inc=True):
                act.wait_ge(pre_t, n + 1)
                src = pre_bank[n % 2][0:dst.shape[0], 0:cols]
                nc.scalar.activation(dst, src, ACT.Copy, scale=scale).then_inc(pre_a, 1)

            def flat(ap):
                return ap.rearrange("p a b -> p (a b)")

            def before_scores(s):
                if s == 1:
                    emptied(XN, flat(xnT[:, :, :]), cols=DM)
                if s in (2, 4, 6):
                    wk_half(s // 2)
                if 4 <= s < 8:
                    for h in range(GH * (s - 4), GH * (s - 3)):
                        act.wait_ge(q_copied, h // 4 + 1)
                        if h >= 4:
                            act.wait_ge(q_sq, h - 3)
                        nc.scalar.activation(junk_a[:, h % 4, :], q_bank[h // 4 % 2][:, D * (h % 4):D * (h % 4) + D],
                                             ACT.Square, accum_out=qsq[:, h:h + 1]).then_inc(q_sq, 1)
                if s in (9, 10):
                    act.wait_ge(gg_ready, 1)
                    for n in (2 * s - 18, 2 * s - 17):
                        emptied(QT0 + n, flat(qT[:, 4 * n:4 * n + 4, :]), scale=gg_s[:, 0:1])
                if s in (11, 12):
                    for n in (2 * s - 22, 2 * s - 21):
                        emptied(U0 + n, flat(u_hi[:, 4 * n:4 * n + 4, :]))
                if s == 15:
                    for n in range(2):
                        act.wait_ge(pre_t, WOUT0 + n + 1)
                        nc.scalar.activation(flat(w_outT[:, 2 * n:2 * n + 2, :]), pre_bank[(WOUT0 + n) % 2][:, :],
                                             ACT.Copy).then_inc(pre_a, 1)
                    act.wait_ge(pre_t, RW0 + 1)
                    nc.scalar.activation(rwT[:, :, :],
                                         pre_bank[RW0 % 2][:, 0:2 * P].rearrange("p (a e) -> p a e", a=2)[:, :, 0:E],
                                         ACT.Copy).then_inc(pre_a, 1)

            def exp_head(h):
                act.wait_ge(nmax_ready, h + 1)
                row = prob[(h // GH) % 2][:, h % GH, :]
                nc.scalar.activation(row, row, ACT.Exp, bias=nmax[:, h:h + 1],
                                     accum_out=psum_[:, h:h + 1]).then_inc(p_ready, 1)

            def leave_ctx(g):
                act.wait_ge(c_done, KT * (g + 1))
                if g == 0:
                    act.wait_ge(k_done, G * KT)
                if g > 0:
                    act.wait_ge(vo_done, g)
                nc.scalar.activation(oT[:, :], c_bank[:, :], ACT.Copy).then_inc(oT_ready, 1)

            def leave_value(g):
                act.wait_ge(voT_done, g + 1)
                if g > 0:
                    act.wait_ge(y_done, g)
                nc.scalar.activation(flat(voT[:, :, :]), v_bank[:, :], ACT.Copy).then_inc(voT_ready, 1)

            def norms_out(g):
                act.wait_ge(rk_turned, g + 1)
                if g > 0:
                    act.wait_ge(rrow_ld, 16 * GH * g)
                nc.scalar.activation(rkT[:, :], norm_bank(g)[0:GH * KT, 0:P], ACT.Copy).then_inc(rkT_ready, 1)

            def gate_up_high(e):
                if e in FIRST_OF:
                    act.wait_ge(ld_exp[FIRST_OF[e]], 64)
                if e == 0:
                    act.wait_ge(c_done, G * KT)
                if e >= WS:
                    act.wait_ge(gu_done, e - WS + 1)
                nc.scalar.activation(flat(gu_hi[:, e % WS, :, :]), flat(guw[:, e, :, :]), ACT.Copy).then_inc(gh_ready, 1)

            for s in range(SLOTS):
                k, su, cu = s, s - S_AT, s - C_AT
                before_scores(s)
                for half in range(2):
                    if 0 <= cu < G * UNITS:
                        m = 2 * cu + half
                        act.wait_ge(t_done, m + 1)
                        if m >= PT:
                            act.wait_ge(c_done, m - PT + 1)
                        nc.scalar.activation(pT_hi[:, m % PT, :], t_bank[m % 2][:, :], ACT.Copy).then_inc(hi_done, 1)
                        if m % KT == 1 and m > KT:
                            leave_ctx(m // KT - 1)
                    if half == 0 and su > 0 and su % 2 == 0 and su <= G * UNITS:
                        exp_head(su // 2 - 1)
                if s % UNITS == R_TURN and 0 < s // UNITS <= G:
                    norms_out(s // UNITS - 1)
                if k < G * UNITS:
                    g, t = k // UNITS, 2 * (k % UNITS)
                    act.wait_ge(k_done, KT * g + t + 1)
                    for j in range(GH):
                        kj = k_home(KT * g + t)[:, D * j:D * j + D]
                        last = nc.scalar.activation(kj, kj, ACT.Square, accum_out=ssq[:, g, j, t:t + 1])
                    last.then_inc(k_sq, 1)
                if cu >= UNITS and cu % UNITS == V_AT + 1:
                    leave_value(cu // UNITS - 1)
                if s == G * UNITS + 10:
                    act.wait_ge(dt_neg, 1)
                    nc.scalar.activation(dt_sb[:, :], dt_sb[:, :], ACT.Exp, bias=dstat[:, 0:1], scale=-1.0,
                                         accum_out=dstat[:, 1:2]).then_inc(dt_exp, 1)
            leave_ctx(G - 1)
            leave_value(G - 1)

            nc.scalar.preload_act_table(ACT.Sigmoid)
            for e in range(WS):
                gate_up_high(e)
            act.wait_ge(t2, 2)
            act.wait_ge(ld_gb, 64)
            nc.scalar.activation(x2T[:, 1, :], x_bank[1][:, 0:T], ACT.Identity, bias=beta_c[:, 1:2],
                                 scale=gamma_c[:, 1:2]).then_inc(a2_a, 1)
            act.wait_ge(clip_done, 1)
            nc.scalar.activation(sg[:, 1, :], zc[:, 1, :], ACT.Sigmoid).then_inc(sig_done, 1)
            for i in range(2):
                act.wait_ge(clip_done, i + 2)
                c0 = slice(i * DI // 2, (i + 1) * DI // 2)
                nc.scalar.activation(sg[:, 0, c0], zc[:, 0, c0], ACT.Sigmoid).then_inc(sig_done, 1)
            nc.scalar.preload_act_table(ACT.Exp)
            for i in range(2):
                act.wait_ge(ooT_done, i + 1)
                nc.scalar.activation(flat(ooT[:, 2 * i:2 * i + 2, :]), x_bank[i][:, 0:2 * P], ACT.Copy).then_inc(ooT_ready, 1)
            act.wait_ge(t2, 3)
            nc.scalar.activation(flat(xmT[:, :, :]), d_bank[:, 0:DM], ACT.Copy).then_inc(a2_a, 1)
            nc.scalar.activation(flat(xmT_hi[:, :, :]), d_bank[:, 0:DM], ACT.Copy).then_inc(xh_ready, 1)
            act.wait_ge(lg_max, 1)
            nc.scalar.activation(ex[:, :], lg[:, :], ACT.Exp, bias=lstat[:, 1:2]).then_inc(lg_exp, 1)
            nc.scalar.preload_act_table(ACT.Silu)
            for e in range(E + 1):
                if e < E:
                    act.wait_ge(gu_done, e + 1)
                    if e >= 2:
                        act.wait_ge(act_ready, e - 1)
                    nc.scalar.activation(silu_g[:, e % 2, :], gu_bank[e % GU][:, 0:I], ACT.Silu).then_inc(silu_done, 1)
                if e >= 1:
                    act.wait_ge(at_done, e)
                    if e >= 3:
                        act.wait_ge(dn_done, e - 2)
                    nc.scalar.activation(flat(actT_hi[:, (e - 1) % 2, :, :]), a_bank[(e - 1) % 2][0:IH, 0:2 * T],
                                         ACT.Copy).then_inc(ah_ready, 1)
                    if e - 1 + WS < E:
                        gate_up_high(e - 1 + WS)

        @block.vector
        def _(dve):
            steps = [0]

            def link(ins):
                steps[0] += 1
                ins.then_inc(dve_seq, 1)
                dve.wait_ge(dve_seq, steps[0])

            def rsqrt(y, v, t, done):
                link(nc.vector.tensor_scalar(out=y.bitcast(I32), in0=v.bitcast(I32), scalar1=1, scalar2=None,
                                             op0=ALU.logical_shift_right))
                link(nc.vector.tensor_scalar(out=y.bitcast(I32), in0=y.bitcast(I32), scalar1=-1.0,
                                             scalar2=float(0x5F3759DF), op0=ALU.mult, op1=ALU.add))
                for step in range(3):
                    link(nc.vector.scalar_tensor_tensor(out=t, in0=y, scalar=-0.5, in1=y, op0=ALU.mult, op1=ALU.mult))
                    link(nc.vector.tensor_tensor(out=t, in0=t, in1=v, op=ALU.mult))
                    last = nc.vector.scalar_tensor_tensor(out=y, in0=t, scalar=1.5, in1=y, op0=ALU.add, op1=ALU.mult)
                    if step < 2:
                        link(last)
                last.then_inc(done, 1)

            def ln_stats(n, src):
                link(nc.vector.bn_stats(out=stat[:, :], in_=src))
                link(nc.vector.bn_aggr(out=mv[:, :], in_=stat[:, :]))
                nc.vector.tensor_scalar(out=mv[:, 1:2], in0=mv[:, 1:2], scalar1=EPS, scalar2=None,
                                        op0=ALU.add).then_inc(var_ready, 1)
                dve.wait_ge(rstd_ready, n + 1)

            def normed(dst, src):
                return nc.vector.tensor_scalar(out=dst, in0=src, scalar1=mv[:, 0:1], scalar2=rstd[:, 0:1],
                                               op0=ALU.subtract, op1=ALU.mult)

            def flat(ap):
                return ap.rearrange("p a b -> p (a b)")

            def wk_low(i):
                c0 = slice(i * BANK, i * BANK + BANK)
                dve.wait_ge(wk_hi_done, i + 1)
                nc.vector.tensor_tensor(out=wk_lo[:, c0], in0=wk_sb[:, c0], in1=wk_hi[:, c0].bitcast(F32),
                                        op=ALU.subtract).then_inc(wk_lo_done, 1)

            for i in range(4):
                c0 = slice(i * BANK, i * BANK + BANK)
                if i == 1:
                    wk_low(0)
                dve.wait_ge(pre_a, i + 1)
                nc.vector.tensor_tensor(out=ctxT_lo[:, c0], in0=pre_bank[i % 2][:, :],
                                        in1=ctxT_hi[:, c0].bitcast(F32), op=ALU.subtract).then_inc(pre_v, 1)
                if i == 3:
                    dve.wait_ge(ld_x, 16)
                    dve.wait_ge(mhalf_made, 1)
                    ln_stats(0, x_sb[:, :])
                    normed(xn[:, :], x_sb[:, :]).then_inc(ln_ready, 1)

            def before_scores(s):
                if s in (2, 3):
                    for n in (2 * s - 4, 2 * s - 3):
                        emptied(WK0 + n, flat(wkT[:, 4 * n:4 * n + 4, :]), pre_bank[(WK0 + n) % 2][:, :])
                if s in (2, 4, 6):
                    wk_low(s // 2)
                if 4 <= s < 8:
                    n = s - 4
                    dve.wait_ge(q_done, n + 1)
                    nc.vector.tensor_copy(q_sb[:, n * BANK:n * BANK + BANK], q_bank[n % 2][:, :]).then_inc(q_copied, 1)
                if s == 8:
                    dve.wait_ge(ld_g, 32)
                    nc.vector.scalar_tensor_tensor(out=gg_s[:, :], in0=gcol[:, 0:1], scalar=float(D) ** -0.5,
                                                   in1=gcol[:, 1:2], op0=ALU.mult, op1=ALU.mult).then_inc(gg_ready, 1)
                    dve.wait_ge(q_sq, H)
                    link(nc.vector.tensor_scalar(out=qsq[:, :], in0=qsq[:, :], scalar1=1.0 / D, scalar2=EPS,
                                                 op0=ALU.mult, op1=ALU.add))
                    rsqrt(rq[:, :], qsq[:, :], ta[:, 0:H], rq_ready)
                    dve.wait_ge(rq_ready, 1)
                    for n in range(4):
                        q4 = q_sb[:, n * BANK:n * BANK + BANK].rearrange("p (h d) -> p h d", d=D)
                        nc.vector.tensor_tensor(
                            out=q4, in0=q4, in1=rq[:, 4 * n:4 * n + 4].unsqueeze(2).to_broadcast([T, 4, D]),
                            op=ALU.mult).then_inc(q_norm, 1)
                if s in (11, 12):
                    for n in (2 * s - 22, 2 * s - 21):
                        dve.wait_ge(pre_a, by(U0 + n, "a"))
                        nc.vector.tensor_tensor(out=flat(u_lo[:, 4 * n:4 * n + 4, :]), in0=pre_bank[(U0 + n) % 2][:, :],
                                                in1=flat(u_hi[:, 4 * n:4 * n + 4, :]).bitcast(F32),
                                                op=ALU.subtract).then_inc(pre_v, 1)

                if s in (13, 14):
                    for n in (2 * s - 26, 2 * s - 25):
                        emptied(WIN0 + n, w_inT[:, :, 256 * n:256 * n + 256].rearrange("p a (j e) -> p a j e", j=2),
                                pre_bank[(WIN0 + n) % 2][:, :].rearrange("p (j a e) -> p a j e", j=2, a=2))

            def emptied(n, dst, src):
                dve.wait_ge(pre_t, n + 1)
                nc.vector.tensor_copy(dst, src).then_inc(pre_v, 1)

            def k_stats(k):
                g, t = k // UNITS, 2 * (k % UNITS) + 1
                dve.wait_ge(k_done, KT * g + t + 1)
                if g > 1 and t == 1:
                    dve.wait_ge(kv_ready, g - 1)
                for j in range(GH):
                    last = nc.vector.bn_stats(out=bn[:, g % 2, j, t // 2, :], in_=k_home(KT * g + t)[:, D * j:D * j + D])
                last.then_inc(k_bn, 1)

            def key_norms(g):
                dve.wait_ge(kv_ready, g + 1)
                rsqrt(rk[:, g, :, :].rearrange("p h t -> p (h t)"), ssq[:, g, :, :].rearrange("p h t -> p (h t)"),
                      ta[:, :], rk_ready)

            def scaled_scores(u, c2):
                h, c = u // 2, 2 * (u % 2) + c2
                n = NC * h + c
                g, j = h // GH, h % GH
                dve.wait_ge(s_done, n + 1)
                dve.wait_ge(rbc_ready, h + 1)
                if c == 0 and j == 0 and g >= 2:
                    dve.wait_ge(t_done, KT * (g - 1))
                c0 = slice(c * BANK, c * BANK + BANK)
                nc.vector.tensor_tensor_reduce(out=prob[g % 2][:, j, c0], in0=s_bank[n % 3][:, :],
                                               in1=rbc[h % 2][:, c0], scale=1.0, scalar=-3.0e38, op0=ALU.mult,
                                               op1=ALU.max, accum_out=smax[:, h, c:c + 1]).then_inc(sr_done, 1)
                if c == NC - 1:
                    dve.wait_ge(sr_done, n + 1)
                    link(nc.vector.tensor_reduce(out=pmax[:, h:h + 1], in_=smax[:, h, :], axis=AX.X, op=ALU.max))
                    nc.vector.tensor_scalar(out=nmax[:, h:h + 1], in0=pmax[:, h:h + 1], scalar1=-1.0, scalar2=None,
                                            op0=ALU.mult).then_inc(nmax_ready, 1)

            def scaled_value(g):
                h0 = GH * g
                dve.wait_ge(p_ready, h0 + GH)
                link(nc.vector.reciprocal(out=rs[:, h0:h0 + GH], in_=psum_[:, h0:h0 + GH]))
                dve.wait_ge(vo_done, g + 1)
                if g > 0:
                    dve.wait_ge(voT_done, g)
                nc.vector.tensor_tensor(out=vo_sb[:, :].rearrange("p (h d) -> p h d", d=D),
                                        in0=v_bank[:, :].rearrange("p (h d) -> p h d", d=D),
                                        in1=rs[:, h0:h0 + GH].unsqueeze(2).to_broadcast([T, GH, D]),
                                        op=ALU.mult).then_inc(vo_ready, 1)

            def gate_up_low(e):
                if e == 0:
                    dve.wait_ge(y_done, G)
                dve.wait_ge(gh_ready, e + 1)
                if e >= WS:
                    dve.wait_ge(gu_done, e - WS + 1)
                nc.vector.tensor_tensor(out=flat(gu_lo[:, e % WS, :, :]), in0=flat(guw[:, e, :, :]),
                                        in1=flat(gu_hi[:, e % WS, :, :]).bitcast(F32),
                                        op=ALU.subtract).then_inc(gl_ready, 1)

            def clip(dst, src):
                nc.vector.tensor_scalar(out=dst, in0=src, scalar1=15.0, scalar2=-15.0, op0=ALU.min,
                                        op1=ALU.max).then_inc(clip_done, 1)

            for s in range(SLOTS):
                k, su, cu = s, s - S_AT, s - C_AT
                before_scores(s)
                for half in range(2):
                    if 0 <= cu < G * UNITS:
                        m = 2 * cu + half
                        dve.wait_ge(hi_done, m + 1)
                        nc.vector.tensor_tensor(out=pT_lo[:, m % PT, :], in0=t_bank[m % 2][:, :],
                                                in1=pT_hi[:, m % PT, :].bitcast(F32), op=ALU.subtract).then_inc(lo_done, 1)
                    if 0 <= su < G * UNITS:
                        scaled_scores(su, half)
                if k < G * UNITS:
                    k_stats(k)
                if s % UNITS == N_AT and 0 < s // UNITS <= G:
                    key_norms(s // UNITS - 1)
                if s == G * UNITS + 8:
                    dve.wait_ge(ld_dt, 16)
                    nc.vector.tensor_reduce(out=dstat[:, 0:1], in_=dt_sb[:, :], axis=AX.X,
                                            op=ALU.min).then_inc(dt_neg, 1)
                if s == G * UNITS + 12:
                    dve.wait_ge(dt_exp, 1)
                    link(nc.vector.reciprocal(out=dstat[:, 2:3], in_=dstat[:, 1:2]))
                    link(nc.vector.tensor_scalar(out=dt_sb[:, :], in0=dt_sb[:, :], scalar1=dstat[:, 2:3], scalar2=None,
                                                 op0=ALU.mult))
                if cu >= UNITS and cu % UNITS == V_AT:
                    scaled_value(cu // UNITS - 1)
            scaled_value(G - 1)

            dve.wait_ge(y_done, G)
            dve.wait_ge(c_done, G * KT)
            link(nc.vector.tensor_tensor(out=x1[:, :], in0=x_sb[:, :], in1=y_bank[:, 0:DM], op=ALU.add))
            ln_stats(1, x1[:, :])
            normed(y1[:, :], x1[:, :]).then_inc(ln_ready, 1)
            dve.wait_ge(ln_ready, 2)
            ln_stats(2, y1[:, :])
            normed(xn2[:, :], y1[:, :]).then_inc(ln_ready, 1)
            nc.vector.tensor_tensor(out=s1[:, :], in0=x1[:, :], in1=y1[:, :], op=ALU.add).then_inc(s1_ready, 1)
            dve.wait_ge(t2, 1)
            dve.wait_ge(ld_gb, 64)
            nc.vector.tensor_scalar(out=x2T[:, 0, :], in0=x_bank[0][:, 0:T], scalar1=gamma_c[:, 0:1],
                                    scalar2=beta_c[:, 0:1], op0=ALU.mult, op1=ALU.add).then_inc(a2_v, 1)
            gate_up_low(0)
            dve.wait_ge(pr_done, 1)
            clip(zc[:, 1, :], g_bank[:, :])
            dve.wait_ge(clip_done, 1)
            link(nc.vector.tensor_tensor(out=gg[:, :], in0=zc[:, 1, :], in1=dt_sb[:, :], op=ALU.mult))
            dve.wait_ge(sig_done, 1)
            link(nc.vector.tensor_tensor(out=gg[:, :], in0=gg[:, :], in1=sg[:, 1, :], op=ALU.mult))
            for i in range(2):
                c0 = slice(i * DI // 2, (i + 1) * DI // 2)
                dve.wait_ge(pr_done, i + 2)
                clip(zc[:, 0, c0], z_bank[i][:, 0:DI // 2])
                link(nc.vector.tensor_tensor(out=zz[:, c0], in0=z_bank[i][:, 0:DI // 2], in1=gg[:, c0], op=ALU.mult))
                dve.wait_ge(sig_done, i + 2)
                nc.vector.tensor_tensor(out=oo[:, c0], in0=zz[:, c0], in1=sg[:, 0, c0], op=ALU.mult).then_inc(oo_ready, 1)
            gate_up_low(1)
            gate_up_low(2)
            dve.wait_ge(s1_ready, 1)
            dve.wait_ge(mo_done, 1)
            link(nc.vector.tensor_tensor(out=x2[:, :], in0=o_bank[:, 0:DM], in1=s1[:, :], op=ALU.add))
            ln_stats(3, x2[:, :])
            normed(xm[:, :], x2[:, :]).then_inc(ln_ready, 1)

            dve.wait_ge(xh_ready, 1)
            nc.vector.tensor_tensor(out=flat(xmT_lo[:, :, :]), in0=flat(xmT[:, :, :]),
                                    in1=flat(xmT_hi[:, :, :]).bitcast(F32), op=ALU.subtract).then_inc(xl_ready, 1)

            dve.wait_ge(lg_done, 1)
            dve.wait_ge(ld_bias, 16)
            link(nc.vector.tensor_tensor(out=lg[:, :], in0=l_bank[:, 0:E], in1=bias_bc[:, :], op=ALU.add))
            link(nc.vector.tensor_reduce(out=lstat[:, 0:1], in_=lg[:, :], axis=AX.X, op=ALU.max))
            nc.vector.tensor_scalar(out=lstat[:, 1:2], in0=lstat[:, 0:1], scalar1=-1.0, scalar2=None,
                                    op0=ALU.mult).then_inc(lg_max, 1)
            dve.wait_ge(lg_exp, 1)
            dve.wait_ge(before_made, 2)
            other = ex[:, :].unsqueeze(1).to_broadcast([T, E, E])
            own = ex[:, :].unsqueeze(2).to_broadcast([T, E, E])
            link(nc.vector.tensor_tensor(out=cmp_a[:, :, :], in0=other, in1=own, op=ALU.is_equal))
            link(nc.vector.tensor_tensor(out=cmp_a[:, :, :], in0=cmp_a[:, :, :], in1=before[:, :, :], op=ALU.mult))
            link(nc.vector.tensor_tensor(out=cmp_b[:, :, :], in0=other, in1=own, op=ALU.is_gt))
            link(nc.vector.tensor_tensor(out=cmp_a[:, :, :], in0=cmp_a[:, :, :], in1=cmp_b[:, :, :], op=ALU.add))
            link(nc.vector.tensor_reduce(out=rank[:, :], in_=cmp_a[:, :, :], axis=AX.X, op=ALU.add))
            link(nc.vector.scalar_tensor_tensor(out=top[:, :], in0=rank[:, :], scalar=float(TOP_K), in1=ex[:, :],
                                                op0=ALU.is_lt, op1=ALU.mult))
            link(nc.vector.tensor_reduce(out=lstat[:, 2:3], in_=top[:, :], axis=AX.X, op=ALU.add))
            link(nc.vector.reciprocal(out=lstat[:, 3:4], in_=lstat[:, 2:3]))
            link(nc.vector.tensor_scalar(out=wgt[:, :], in0=top[:, :], scalar1=lstat[:, 3:4], scalar2=None, op0=ALU.mult))
            for e in range(E + 1):
                if e < E:
                    dve.wait_ge(silu_done, e + 1)
                    if e >= 2:
                        dve.wait_ge(at_done, e - 1)
                    nc.vector.scalar_tensor_tensor(out=acts[:, e % 2, :], in0=silu_g[:, e % 2, :],
                                                   scalar=wgt[:, e:e + 1], in1=gu_bank[e % GU][:, I:2 * I],
                                                   op0=ALU.mult, op1=ALU.mult).then_inc(act_ready, 1)
                if e >= 1:
                    dve.wait_ge(ah_ready, e)
                    nc.vector.tensor_tensor(out=flat(actT_lo[:, (e - 1) % 2, :, :]),
                                            in0=a_bank[(e - 1) % 2][0:IH, 0:2 * T],
                                            in1=flat(actT_hi[:, (e - 1) % 2, :, :]).bitcast(F32),
                                            op=ALU.subtract).then_inc(al_ready, 1)
                    if e - 1 + WS < E:
                        gate_up_low(e - 1 + WS)
            dve.wait_ge(dn_done, E)
            nc.vector.tensor_tensor(out=x3[:, :], in0=d_bank[:, 0:DM], in1=x2[:, :], op=ALU.add).then_inc(x3_ready, 1)


_INS = ['x', 'ctx_1024', 'L0_xattn_Wq', 'L0_xattn_Wk', 'L0_xattn_Wv', 'L0_xattn_Wo', 'L0_xattn_gq', 'L0_xattn_gk',
        'L0_attn_gamma', 'L0_attn_beta', 'L0_attn_W_in', 'L0_attn_W_out', 'L0_attn_dt', 'L0_ffn_router_w',
        'L0_ffn_expert_bias', 'L0_ffn_gate_proj', 'L0_ffn_up_proj', 'L0_ffn_down_proj']


def kernel(**inputs):
    import numpy as _np
    import concourse.bacc as _bacc
    from concourse import mybir as _mybir
    from concourse.bass_utils import run_bass_kernel_spmd as _run

    nc = _bacc.Bacc("TRN2", target_bir_lowering=False, num_devices=1)
    arrays, args = {}, []
    for name in _INS:
        a = _np.ascontiguousarray(inputs[name])
        arrays[f"in_{name}"] = a
        args.append(nc.dram_tensor(f"in_{name}", a.shape, _mybir.dt.from_np(a.dtype), kind="ExternalInput").ap())
    shape = inputs['x'].shape
    args.append(nc.dram_tensor("out_0", shape, _mybir.dt.float32, kind="ExternalOutput").ap())
    perceiver_layer(nc, *args)
    r = _run(nc, [arrays], core_ids=[0])
    return r.results[0]["out_0"]
```

```python
import concourse.bass as bass
from concourse import mybir

F32 = mybir.dt.float32
F32R = mybir.dt.float32r
I32 = mybir.dt.int32
ALU = mybir.AluOpType
ACT = mybir.ActivationFunctionType
AX = mybir.AxisListType

P = 128
EPS = 1e-5


def perceiver_layer(nc, x, ctx, Wq, Wk, Wv, Wo, gq, gk, gamma, beta, W_in, W_out, dt, router_w,
                    expert_bias, gate_proj, up_proj, down_proj, out):
    T, DM = x.shape[1], x.shape[2]
    NKEY, C = ctx.shape[1], ctx.shape[2]
    D = gq.shape[0]
    H = Wq.shape[1] // D
    KT = NKEY // P
    GH = 4
    G = H // GH
    BANK = 512
    NC = NKEY // BANK
    DI = dt.shape[0]
    E, I = gate_proj.shape[0], gate_proj.shape[2]
    IH = I // 2
    DA = DM // P
    TOP_K = 4
    HI = DI // 2
    PT = 3
    WS, DS = 5, 3
    EW = 2
    LL = 2
    TL = 2
    AD = 3
    GU = 4

    UNITS = KT // 2
    S_AT = 2 * UNITS
    C_AT = S_AT + UNITS + 2
    SLOTS = C_AT + G * UNITS
    N_AT = 1
    R_TURN = 5
    V_AT = 4
    WARM = (5, 3, 3)
    E_AT = (SLOTS - 4, SLOTS - 1)
    WK_AT = (4, 6, 16)
    EARLY = 2 * UNITS

    KB = 1024
    base = (nc.sbuf_base + 31) // 32 * 32

    def at(name, shape, kb, dtype=F32):
        return nc.alloc_sbuf_tensor_at(name, shape, dtype, offset=base + int(kb * KB))

    ctx_hi = at("ctx_hi", [P, KT, C], 0, F32R)
    ctx_lo = at("ctx_lo", [P, KT, C], 8, F32R)
    ctxT_hi = at("ctxT_hi", [C, NKEY], 16, F32R)
    ctxT_lo = at("ctxT_lo", [C, NKEY], 24, F32R)
    wk_hi = at("wk_hi", [C, H * D], 32, F32R)
    wk_lo = at("wk_lo", [C, H * D], 40, F32R)
    u_hi = at("u_hi", [C, H, T], 48, F32R)
    u_lo = at("u_lo", [C, H, T], 56, F32R)
    prob = [at(f"prob{i}", [T, GH, NKEY], 64 + 32 * i) for i in range(2)]
    rbc = [at(f"rbc{i}", [P, NKEY], 128 + 8 * i) for i in range(2)]
    rrow = at("rrow", [P, NKEY], 144)
    pT_hi = at("pT_hi", [P, PT, BANK], 152, F32R)
    pT_lo = at("pT_lo", [P, PT, BANK], 158, F32R)
    wv = at("wv", [C, H * D], 164)
    wo = at("wo", [D, H, DM], 172)
    w_in_sb = at("w_in_sb", [P, 2 * DI // P, DM], 188)
    w_out_sb = at("w_out_sb", [P, DA, DI], 196)
    small = [200.0]

    def tiny(name, shape, dtype=F32):
        n = 4
        for d in shape[1:]:
            n *= d
        t = at(name, shape, small[0], dtype)
        small[0] += (n + 31) // 32 * 32 / KB
        return t

    wq_sb = at("wq_sb", [P, DA, H * D], 64)
    q_sb = at("q_sb", [T, H * D], 80)
    qT = at("qT", [D, H, T], 88)
    wk_sb = at("wk_sb", [C, H * D], 96)
    wkT = at("wkT", [D, H, C], 104)
    junk_a = at("junk_a", [P, 4, D], 124)
    xn = at("xn", [T, DM], 126)
    xnT = at("xnT", [P, DA, T], 127)
    rw_sb = at("rw_sb", [E, DM], 152)
    ctx_sb = at("ctx_sb", [P, KT, C], 128)
    oT = at("oT", [C, GH * T], 32)
    x1 = at("x1", [T, DM], 34)
    voT = at("voT", [D, GH, T], 36)
    dt_sb = at("dt_sb", [P, DI], 38)
    dt_c = at("dt_c", [P, DI // P], 42.5)
    EXPERTS = ((0, 6), (6, 10), (10, E))
    guw_parts = [at(f"guw{n}", [P, hi - lo, DA, 2 * I], kb)
                 for n, ((lo, hi), kb) in enumerate(zip(EXPERTS, (129, 48, 96)))]
    dww = at("dww", [IH, E, 2, DM], 64)
    y1 = at("y1", [T, DM], 1)
    s1 = at("s1", [T, DM], 2)
    xn2 = at("xn2", [T, DM], 3)
    x2 = at("x2", [T, DM], 4)
    xm = at("xm", [T, DM], 5)
    x2T = at("x2T", [P, DA, T], 6)
    xmT = at("xmT", [P, DA, T], 7)
    zc = at("zc", [T, 2, DI], 8)
    sg = at("sg", [T, 2, DI], 12)
    w_inT = at("w_inT", [P, DA, 2 * DI], 152)
    w_outT = at("w_outT", [P, DI // P, DM], 160)
    zz = at("zz", [T, DI], 188)
    gg = at("gg", [T, DI], 190)
    oo = at("oo", [T, DI], 192)
    ooT = at("ooT", [P, DI // P, T], 194)
    silu_g = at("silu_g", [T, 2, I], 160)
    acts = at("acts", [T, AD, I], 8)
    xmT_hi = at("xmT_hi", [P, DA, T], 43, F32R)
    xmT_lo = at("xmT_lo", [P, DA, T], 44, F32R)
    actT_hi = at("actT_hi", [IH, 2, 2, T], 45, F32R)
    actT_lo = at("actT_lo", [IH, 2, 2, T], 32, F32R)
    GU_AT = (16, 23, 164, 171, 178)
    gu_hi = [at(f"gu_hi{i}", [P, DA, 2 * I], kb, F32R) for i, kb in enumerate(GU_AT)]
    gu_lo = [at(f"gu_lo{i}", [P, DA, 2 * I], kb + 3.5, F32R) for i, kb in enumerate(GU_AT)]
    dw_hi = at("dw_hi", [IH, DS, 2, DM], 117, F32R)
    dw_lo = at("dw_lo", [IH, DS, 2, DM], 123, F32R)
    x3 = at("x3", [T, DM], 162)

    ident = tiny("ident", [P, P])
    x_sb = tiny("x_sb", [T, DM])
    ssq = tiny("ssq", [P, G, GH, KT])
    bn = tiny("bn", [P, 2, GH, UNITS, 6])
    rk = tiny("rk", [P, G, GH, KT])
    ta = tiny("ta", [P, GH * KT])
    tb = tiny("tb", [P, GH * KT])
    rkT = tiny("rkT", [GH * KT, P])
    qsq = tiny("qsq", [T, H])
    rq = tiny("rq", [T, H])
    gcol = tiny("gcol", [D, 2])
    gg_s = tiny("gg_s", [D, 1])
    gamma_c = tiny("gamma_c", [P, DA])
    beta_c = tiny("beta_c", [P, DA])
    stat = tiny("stat", [T, 6])
    mv = tiny("mv", [T, 2])
    rstd = tiny("rstd", [T, 1])
    mhalf = tiny("mhalf", [P, 1])
    smax = tiny("smax", [T, H, NC])
    nmax = tiny("nmax", [T, H])
    pmax = tiny("pmax", [T, H])
    psum_ = tiny("psum_", [T, H + 4])
    rs = tiny("rs", [T, H])
    rwT = tiny("rwT", [P, DA, E])
    bias_bc = tiny("bias_bc", [P, E])
    dstat = tiny("dstat", [P, 4])
    lg = tiny("lg", [T, E])
    ex = tiny("ex", [T, E])
    rank = tiny("rank", [T, E])
    top = tiny("top", [T, E])
    lstat = tiny("lstat", [T, 4])
    cmp_a = at("cmp_a", [T, E, E], 41)
    cmp_b = at("cmp_b", [T, E, E], 35)
    before = at("before", [P, E, E], 40)
    assert base + small[0] * KB <= nc.sbuf_usable_end, small[0]

    bank = [nc.alloc_psum_tensor(f"bank{i}", [P, BANK], F32) for i in range(8)]
    k_bank = bank[0:4]
    s_bank = (bank[4], bank[2], bank[3])
    t_bank = bank[5:7]
    EXP_PARTS = 4
    HALF = GH * T // 2

    def c_bank(g):
        return bank[7] if g < G - 1 else bank[4]

    q_bank = [bank[4], bank[5]]
    pre_bank = [bank[6], bank[7]]

    def v_home(g, j):
        if g < G - 1 or j < GH // 2:
            return bank[0][:, T * j:T * j + T]
        return bank[5][:, T * (j - GH // 2):T * (j - GH // 2) + T]

    def t_home(m, j):
        if m < G * KT - 1 or j < GH // 2:
            return t_bank[m % 2][:, T * j:T * j + T]
        return bank[3][:, T * (j - GH // 2):T * (j - GH // 2) + T]

    def y_home(g, j):
        if g < G - 1:
            return bank[1 - j // 2][:, DM * (j % 2):DM * (j % 2) + DM]
        return bank[1 + j][:, 0:DM]

    def y_count(g, j):
        return 2 * g + (1 + j // 2 if g < G - 1 else 1 + j)

    x_bank, g_bank, z_bank, o_bank = (bank[2], bank[5]), (bank[3], bank[1]), (bank[4], bank[0]), bank[6]
    gu_bank, a_bank, d_bank, l_bank = bank[1:1 + GU], bank[5:7], bank[7], bank[0]

    def k_home(n):
        return k_bank[n % 4 if n < 2 * EARLY else n % 2]

    def norm_bank(g):
        return q_bank[1] if g < 2 else k_bank[0]

    def k_before(n):
        return n // 2 - 1 if n < 2 * EARLY + 2 else n // 2

    FIRST_OF = {lo: n for n, (lo, hi) in enumerate(EXPERTS)}

    def sem(name):
        return nc.alloc_semaphore(name)

    ld_x, ld_wq, ld_g, ld_win, ld_wout, ld_gb = map(sem, (
        "ld_x", "ld_wq", "ld_g", "ld_win", "ld_wout", "ld_gb"))
    ld_rw, ld_bias, ld_wv, ld_wo, ld_dt = map(sem, ("ld_rw", "ld_bias", "ld_wv", "ld_wo", "ld_dt"))
    ld_ctx = [sem(f"ld_ctx{i}") for i in range(4)]
    ld_wk = [sem(f"ld_wk{i}") for i in range(2)]
    ld_exp = [sem(f"ld_exp{i}") for i in range(3)]
    ld_dw = sem("ld_dw")
    ident_made, mhalf_made, before_made = map(sem, ("ident_made", "mhalf_made", "before_made"))
    ctx_hi_done, ctx_lo_done = map(sem, ("ctx_hi_done", "ctx_lo_done"))
    pre_t, pre_a, pre_v = map(sem, ("pre_t", "pre_a", "pre_v"))
    wk_hi_done, wk_lo_done = map(sem, ("wk_hi_done", "wk_lo_done"))
    k_done, k_sq, k_bn, rk_ready, rk_turned, rkT_ready, rrow_ld, rbc_ready = map(sem, (
        "k_done", "k_sq", "k_bn", "rk_ready", "rk_turned", "rkT_ready", "rrow_ld", "rbc_ready"))
    var_ready, rstd_ready, ln_ready = map(sem, ("var_ready", "rstd_ready", "ln_ready"))
    q_done, q_sq, q_norm, u_done = map(sem, ("q_done", "q_sq", "q_norm", "u_done"))
    s_done, sr_done, nmax_ready, p_ready = map(sem, ("s_done", "sr_done", "nmax_ready", "p_ready"))
    t_done, hi_done, lo_done, c_done, oT_ready = map(sem, (
        "t_done", "hi_done", "lo_done", "c_done", "oT_ready"))
    vo_done, voT_ready, y_done, y_added = map(sem, ("vo_done", "voT_ready", "y_done", "y_added"))
    xT_out_a, xT_out_v, s1_ready, xh_ready, xl_ready, gh_ready, gl_ready, ah_ready, al_ready, dh_ready, dl_ready = map(sem, (
        "xT_out_a", "xT_out_v", "s1_ready", "xh_ready", "xl_ready", "gh_ready", "gl_ready", "ah_ready", "al_ready",
        "dh_ready", "dl_ready"))
    xT_turned, pr_done, clip_done, sig_done, oo_ready, ooT_done, ooT_ready, mo_done = map(sem, (
        "xT_turned", "pr_done", "clip_done", "sig_done", "oo_ready", "ooT_done", "ooT_ready", "mo_done"))
    dt_neg, dt_exp, lg_done, lg_max, lg_exp = map(sem, ("dt_neg", "dt_exp", "lg_done", "lg_max", "lg_exp"))
    gu_done, silu_done, act_ready, at_done, dn_done, x3_ready, stored = map(sem, (
        "gu_done", "silu_done", "act_ready", "at_done", "dn_done", "x3_ready", "stored"))
    dve_seq, gg_ready, rq_ready, guess_ready = map(sem, ("dve_seq", "gg_ready", "rq_ready", "guess_ready"))
    dtw_ready, gg_done = sem("dtw_ready"), sem("gg_done")
    pool_seq, pool_sq, kv_ready, q_copied = map(sem, ("pool_seq", "pool_sq", "kv_ready", "q_copied"))

    CTX0, XN, WK0, QT0, U0, RW0, WIN0, WOUT0 = 0, 4, 5, 9, 13, 17, 18, 22
    EMPTIER = ["av"] * 4 + ["a"] + ["v", "a"] * 2 + ["a"] * 4 + ["av"] * 4 + ["a"] + ["a", "v", "a", "a"] + ["a"] * 2

    def by(n, who):
        return sum(who in e for e in EMPTIER[:n + 1])

    Y_ALL = y_count(G - 1, GH - 1)

    block = nc.Block()
    with block:
        def load_experts(eng, n):
            (lo, hi), w = EXPERTS[n], guw_parts[n]
            gv = gate_proj.rearrange("e (a p) i -> p e a i", p=P)
            uv = up_proj.rearrange("e (a p) i -> p e a i", p=P)
            for a in range(DA):
                eng.dma_start(w[:, :, a, 0:I], gv[:, lo:hi, a, :]).then_inc(ld_exp[n], 16)
                eng.dma_start(w[:, :, a, I:2 * I], uv[:, lo:hi, a, :]).then_inc(ld_exp[n], 16)

        def gu_loaded(e):
            n = max(n for n, (lo, hi) in enumerate(EXPERTS) if lo <= e)
            return guw_parts[n][:, e - EXPERTS[n][0], :, :].rearrange("p a b -> p (a b)")

        def w_in_place(n):
            return w_inT[:, :, 256 * n:256 * n + 256].rearrange("p a (j e) -> p a j e", j=2)

        def w_in_turned(n):
            return pre_bank[(WIN0 + n) % 2][:, :].rearrange("p (j a e) -> p a j e", j=2, a=2)

        CTX_V = 4

        def rstd_of(pool, n):
            pool.wait_ge(var_ready, n + 1)
            pool.tensor_tensor(out=rstd[:, :], in0=mv[:, 1:2], in1=mhalf[0:T, :], op=ALU.pow).then_inc(rstd_ready, 1)

        @block.sync
        def _(sp):
            ctx_v = ctx[0, :, :].rearrange("(p t) c -> p t c", t=KT)
            for i in range(4):
                sp.dma_start(ctx_sb[:, 4 * i:4 * i + 4, :], ctx_v[:, 4 * i:4 * i + 4, :]).then_inc(ld_ctx[i], 16)
            sp.dma_start(x_sb[:, :], x[0, :, :]).then_inc(ld_x, 16)
            sp.dma_start(wq_sb[:, :, :], Wq.rearrange("(a p) n -> p a n", p=P)).then_inc(ld_wq, 16)
            sp.dma_start(wk_sb[:, BANK:], Wk[:, BANK:]).then_inc(ld_wk[1], 16)
            sp.dma_start(gcol[:, 0:1], gq.rearrange("(p a) -> p a", a=1)).then_inc(ld_g, 16)
            sp.dma_start(gcol[:, 1:2], gk.rearrange("(p a) -> p a", a=1)).then_inc(ld_g, 16)
            sp.dma_start(rw_sb[:, :], router_w).then_inc(ld_rw, 16)
            sp.dma_start(wv[:, :], Wv).then_inc(ld_wv, 16)
            sp.dma_start(wo[:, :, :], Wo.rearrange("(h d) n -> d h n", d=D)).then_inc(ld_wo, 16)
            sp.dma_start(w_in_sb[:, :, :], W_in.rearrange("(j p) d -> p j d", p=P)).then_inc(ld_win, 16)
            sp.dma_start(w_out_sb[:, :, :], W_out.rearrange("(a p) e -> p a e", p=P)).then_inc(ld_wout, 16)
            for a in range(DA):
                for dst, src in ((gamma_c, gamma), (beta_c, beta)):
                    sp.dma_start(dst[:, a:a + 1], src[P * a:P * a + P].rearrange("(p o) -> p o", o=1)).then_inc(ld_gb, 16)
            sp.dma_start(bias_bc[:, :], expert_bias.rearrange("(a e) -> a e", a=1).to_broadcast([P, E])).then_inc(ld_bias, 16)
            for g in range(G):
                sp.wait_ge(rkT_ready, g + 1)
                if g > 0:
                    sp.wait_ge(rbc_ready, GH * g)
                for j in range(GH):
                    sp.dma_start(rrow[32 * j:32 * j + 1, :].rearrange("a (t p) -> a t p", p=P),
                                 rkT[KT * j:KT * j + KT, :]).then_inc(rrow_ld, 16)
            sp.wait_ge(k_done, G * KT)
            sp.dma_start(dt_sb[:, :], dt.rearrange("(a e) -> a e", a=1).to_broadcast([P, DI])).then_inc(ld_dt, 16)
            for n in range(DI // P):
                sp.dma_start(dt_c[:, n:n + 1], dt[P * n:P * n + P].rearrange("(p a) -> p a", a=1)).then_inc(ld_dt, 16)
            sp.wait_ge(sr_done, H * NC)
            load_experts(sp, 0)
            load_experts(sp, 1)
            sp.wait_ge(t_done, 3 * KT)
            down_v = down_proj.rearrange("e (a p) d -> p e a d", p=IH)
            for a in range(2):
                sp.dma_start(dww[:, :, a, :], down_v[:, :, a, :]).then_inc(ld_dw, 16)
            sp.wait_ge(t_done, G * KT + 1)
            load_experts(sp, 2)
            sp.wait_ge(x3_ready, 1)
            sp.dma_start(out[0, :, :], x3[:, :]).then_inc(stored, 16)
            sp.wait_ge(stored, 16)

        def mean_squares(pool, g):
            odd = ssq[:, g, :, :].rearrange("p h (u two) -> p h u two", two=2)[:, :, :, 1]

            def link(ins):
                pool_steps[0] += 1
                ins.then_inc(pool_seq, 1)
                pool.wait_ge(pool_seq, pool_steps[0])

            pool.wait_ge(k_bn, UNITS * (g + 1))
            sq_mean = tb[:, :].rearrange("p (h u two) -> p h u two", h=GH, two=2)
            half = bn[:, g % 2, :, :, :].rearrange("p h u (two f) -> p h u two f", two=2)
            for i in range(2):
                mean_i, m2_i, s_i = half[:, :, :, i, 1], half[:, :, :, i, 2], sq_mean[:, :, :, i]
                nc.gpsimd.tensor_tensor(out=s_i, in0=mean_i, in1=mean_i, op=ALU.mult).then_inc(pool_sq, 1)
            pool.wait_ge(pool_sq, 2 * (g + 1))
            link(nc.gpsimd.tensor_tensor(out=odd, in0=sq_mean[:, :, :, 0], in1=sq_mean[:, :, :, 1], op=ALU.add))
            link(nc.gpsimd.tensor_scalar(out=odd, in0=odd, scalar1=float(D // 2), scalar2=0.0, op0=ALU.mult, op1=ALU.add))
            link(nc.gpsimd.tensor_tensor(out=odd, in0=odd, in1=half[:, :, :, 0, 2], op=ALU.add))
            link(nc.gpsimd.tensor_tensor(out=odd, in0=odd, in1=half[:, :, :, 1, 2], op=ALU.add))
            pool.wait_ge(k_sq, UNITS * (g + 1))
            v = ssq[:, g, :, :].rearrange("p h t -> p (h t)")
            nc.gpsimd.tensor_scalar(out=v, in0=v, scalar1=1.0 / D, scalar2=EPS, op0=ALU.mult,
                                    op1=ALU.add).then_inc(kv_ready, 1)

        def newton(pool, y, v, t, n, done):
            pool.wait_ge(guess_ready, n + 1)
            for step in range(3):
                for i in range(4):
                    if i == 0:
                        last = nc.gpsimd.tensor_tensor(out=t, in0=y, in1=y, op=ALU.mult)
                    if i == 1:
                        last = nc.gpsimd.tensor_tensor(out=t, in0=t, in1=v, op=ALU.mult)
                    if i == 2:
                        last = nc.gpsimd.tensor_scalar(out=t, in0=t, scalar1=-0.5, scalar2=1.5, op0=ALU.mult, op1=ALU.add)
                    if i == 3:
                        last = nc.gpsimd.tensor_tensor(out=y, in0=t, in1=y, op=ALU.mult)
                    if (step, i) != (2, 3):
                        pool_steps[0] += 1
                        last.then_inc(pool_seq, 1)
                        pool.wait_ge(pool_seq, pool_steps[0])
            last.then_inc(done, 1)

        def key_norms(pool, g):
            newton(pool, rk[:, g, :, :].rearrange("p h t -> p (h t)"), ssq[:, g, :, :].rearrange("p h t -> p (h t)"),
                   ta[:, :], g + 1, rk_ready)

        pool_steps = [0]

        @block.gpsimd
        def _(pool):
            pool.memset(ident[:, :], 0.0).then_inc(ident_made, 1)
            pool.wait_ge(ident_made, 1)
            pool.affine_select(out=ident[:, :], in_=ident[:, :], compare_op=ALU.not_equal, fill=1.0, base=0,
                               pattern=[[-1, P]], channel_multiplier=1).then_inc(ident_made, 1)
            pool.memset(mhalf[:, :], -0.5).then_inc(mhalf_made, 1)
            for i in range(4):
                pool.wait_ge(ld_ctx[i], 16)
                t0, t1 = 4 * i, 4 * i + 4
                pool.tensor_scalar(out=ctx_hi[:, t0:t1, :], in0=ctx_sb[:, t0:t1, :], scalar1=1.0, scalar2=0.0,
                                   op0=ALU.mult, op1=ALU.add).then_inc(ctx_hi_done, 1)
                pool.wait_ge(ctx_hi_done, i + 1)
                pool.tensor_tensor(out=ctx_lo[:, t0:t1, :], in0=ctx_sb[:, t0:t1, :],
                                   in1=ctx_hi[:, t0:t1, :].bitcast(F32), op=ALU.subtract).then_inc(ctx_lo_done, 1)
                if i == 1:
                    rstd_of(pool, 0)
            newton(pool, rq[:, :], qsq[:, :], ta[:, 0:H], 0, rq_ready)
            mean_squares(pool, 0)
            key_norms(pool, 0)
            pool.wait_ge(rk_ready, 1)
            for h in range(H):
                g, j = h // GH, h % GH
                pool.wait_ge(rrow_ld, 16 * GH * (g + 1))
                if h >= 2:
                    pool.wait_ge(sr_done, NC * (h - 1))
                if h < 2:
                    pool.wait_ge(pre_v, CTX_V)
                    pool.wait_ge(ctx_lo_done, 4)
                pool.partition_broadcast(rbc[h % 2][:, :], rrow[32 * j:32 * j + 1, :]).then_inc(rbc_ready, 1)
                if j == 1 and g + 1 < G:
                    pool.wait_ge(rbc_ready, h + 1)
                    mean_squares(pool, g + 1)
                    pool.wait_ge(kv_ready, g + 2)
                if j == 2 and g + 1 < G:
                    pool.wait_ge(rbc_ready, h + 1)
                    key_norms(pool, g + 1)
                    pool.wait_ge(rk_ready, g + 2)
            pool.wait_ge(k_done, G * KT)
            pool.memset(before[:, :, :], 1.0).then_inc(before_made, 1)
            pool.wait_ge(before_made, 1)
            pool.affine_select(out=before[:, :, :], in_=before[:, :, :], compare_op=ALU.is_gt, fill=0.0, base=0,
                               pattern=[[1, E], [-1, E]], channel_multiplier=0).then_inc(before_made, 1)
            rstd_of(pool, 1)
            rstd_of(pool, 2)
            pool.wait_ge(t_done, G * KT + 1)
            pool.wait_ge(ld_dw, 32)
            for e in range(E):
                if e >= DS:
                    pool.wait_ge(dn_done, e - DS + 1)
                src, hi, lo = (w[:, i, :, :].rearrange("p a d -> p (a d)") for w, i in (
                    (dww, e), (dw_hi, e % DS), (dw_lo, e % DS)))
                pool.tensor_scalar(out=hi, in0=src, scalar1=1.0, scalar2=0.0, op0=ALU.mult,
                                   op1=ALU.add).then_inc(dh_ready, 1)
                pool.wait_ge(dh_ready, e + 1)
                pool.tensor_tensor(out=lo, in0=src, in1=hi.bitcast(F32), op=ALU.subtract).then_inc(dl_ready, 1)
                if e == 1:
                    rstd_of(pool, 3)

        @block.tensor
        def _(pe):
            def turn(n, pieces, need=None):
                if n >= 2 and "a" in EMPTIER[n - 2]:
                    pe.wait_ge(pre_a, by(n - 2, "a"))
                if n >= 2 and "v" in EMPTIER[n - 2]:
                    pe.wait_ge(pre_v, by(n - 2, "v"))
                for i, emit in enumerate(pieces):
                    last = emit(pre_bank[n % 2], i)
                last.then_inc(pre_t, 1)

            def turned(src, rows=P):
                cols = src.shape[1]
                return lambda b, i: nc.tensor.transpose(b[0:cols, P * i:P * i + rows], src, ident[0:rows, 0:rows])

            def keep_warm(n, moving, dst=bank[7]):
                for _ in range(n):
                    nc.tensor.matmul(dst[:, 0:moving.shape[1]], ident[:, :], moving, start=True, stop=True)

            pe.wait_ge(ident_made, 2)
            keep_warm(WARM[0], ident[:, :])

            def turn_ctx(n):
                pe.wait_ge(ld_ctx[n], 16)
                turn(CTX0 + n, [turned(ctx_sb[:, 4 * n + i, :]) for i in range(4)])

            for n in range(3):
                turn_ctx(n)

            def three_passes(dst, w_hi, w_lo, m_hi, m_lo):
                nc.tensor.matmul(dst, w_hi, m_hi, start=True, stop=False)
                nc.tensor.matmul(dst, w_hi, m_lo, start=False, stop=False)
                return nc.tensor.matmul(dst, w_lo, m_hi, start=False, stop=True)

            def k_unit(s):
                g = s // UNITS
                for t in (2 * (s % UNITS), 2 * (s % UNITS) + 1):
                    n = KT * g + t
                    if k_before(n) > 0:
                        pe.wait_ge((k_sq, k_bn)[t % 2], k_before(n))
                    if g == G - 1 and t == 2 * R_TURN:
                        pe.wait_ge(rkT_ready, g)
                    if t == 0:
                        pe.wait_ge(wk_lo_done, g + 1)
                        pe.wait_ge(wk_hi_done, g + 1)
                    if g == 0 and t % 4 == 0:
                        pe.wait_ge(pre_v, t // 4 + 1)
                        pe.wait_ge(pre_a, t // 4 + 1)
                    c0 = slice(t * P, t * P + P)
                    w0 = slice(g * BANK, g * BANK + BANK)
                    three_passes(k_home(n)[:, :], ctxT_hi[:, c0], ctxT_lo[:, c0],
                                 wk_hi[:, w0], wk_lo[:, w0]).then_inc(k_done, 1)

            def turn_norms(g):
                pe.wait_ge(rk_ready, g + 1)
                if g == 0:
                    pe.wait_ge(q_sq, H)
                if g == 1:
                    pe.wait_ge(rkT_ready, 1)
                if g >= 2:
                    pe.wait_ge(k_sq, min(UNITS * (g + 1) + R_TURN, UNITS * G))
                nc.tensor.transpose(norm_bank(g)[0:GH * KT, 0:P], rk[:, g, :, :].rearrange("p h t -> p (h t)"),
                                    ident[:, :]).then_inc(rk_turned, 1)

            def q_products(n):
                if n == 0:
                    pe.wait_ge(ld_wq, 16)
                    pe.wait_ge(pre_a, by(XN, "a"))
                if n >= 2:
                    pe.wait_ge(q_sq, GH * (n - 1))
                for a in range(DA):
                    last = nc.tensor.matmul(q_bank[n % 2][:, :], xnT[:, a, :], wq_sb[:, a, n * BANK:n * BANK + BANK],
                                            start=(a == 0), stop=(a == DA - 1))
                last.then_inc(q_done, 1)

            def before_scores(s):
                if s == 1:
                    turn_ctx(3)
                if s == 3:
                    pe.wait_ge(ln_ready, 1)
                    turn(XN, [turned(xn[:, P * a:P * a + P]) for a in range(DA)])
                if s in (8, 10):
                    if s == 8:
                        pe.wait_ge(ld_wk[1], 16)
                    for n in (s - 8, s - 7):
                        turn(WK0 + n, [turned(wk_sb[:, P * h:P * h + P]) for h in range(4 * n, 4 * n + 4)])
                if 4 <= s < 8:
                    q_products(s - 4)
                if s in (11, 12):
                    for n in (2 * s - 22, 2 * s - 21):
                        pe.wait_ge(q_norm, n + 1)
                        turn(QT0 + n, [turned(q_sb[:, P * h:P * h + P]) for h in range(4 * n, 4 * n + 4)])
                if s in (13, 14):
                    if s == 13:
                        pe.wait_ge(pre_a, by(QT0 + 3, "a"))
                        pe.wait_ge(pre_v, by(WK0 + 3, "v"))
                    for n in (2 * s - 26, 2 * s - 25):
                        turn(U0 + n, [
                            lambda b, i, h=h: nc.tensor.matmul(b[:, P * i:P * i + T], wkT[:, h, :], qT[:, h, :],
                                                               start=True, stop=True)
                            for h in range(4 * n, 4 * n + 4)])
                if s == 15:
                    pe.wait_ge(ld_rw, 16)
                    turn(RW0, [turned(rw_sb[:, P * a:P * a + P], rows=E) for a in range(DA)])

            def s_chunk(u, c2):
                h, c = u // 2, 2 * (u % 2) + c2
                n = NC * h + c
                if n == 0:
                    pe.wait_ge(pre_a, by(U0 + 3, "a"))
                    pe.wait_ge(pre_v, by(U0 + 3, "v"))
                    pe.wait_ge(q_sq, H)
                if n == 1:
                    pe.wait_ge(k_sq, EARLY)
                if n == 2:
                    pe.wait_ge(k_bn, EARLY)
                if n >= 3:
                    pe.wait_ge(sr_done, n - 2)
                c0 = slice(c * BANK, c * BANK + BANK)
                three_passes(s_bank[n % 3][:, :], u_hi[:, h, :], u_lo[:, h, :],
                             ctxT_hi[:, c0], ctxT_lo[:, c0]).then_inc(s_done, 1)

            def turn_probs(m):
                g, kt = m // KT, m % KT
                if m == 0:
                    pe.wait_ge(pre_a, by(RW0, "a"))
                    pe.wait_ge(rkT_ready, 2)
                if kt == 0 and g < G - 1:
                    pe.wait_ge(p_ready, GH * (g + 1))
                if g == G - 1 and kt % (KT // EXP_PARTS) == 0:
                    pe.wait_ge(p_ready, H + kt // (KT // EXP_PARTS))
                if m >= 2:
                    pe.wait_ge(lo_done, m - 1)
                for j in range(GH):
                    last = nc.tensor.transpose(t_home(m, j), prob[g % 2][:, j, kt * P:kt * P + P], ident[:, :])
                    if j == GH - 1 or m == G * KT - 1 and j == GH // 2 - 1:
                        last.then_inc(t_done, 1)

            def times_ctx(m):
                g, kt = m // KT, m % KT
                if kt == 0 and 0 < g < G - 1:
                    pe.wait_ge(oT_ready, g)
                if kt == 0 and g == G - 1:
                    pe.wait_ge(sr_done, H * NC)
                if m == 0:
                    pe.wait_ge(ctx_lo_done, 4)
                parts = ((0, HALF), (HALF, 2 * HALF)) if m == G * KT - 1 else ((0, 2 * HALF),)
                for n, (c0, c1) in enumerate(parts):
                    pe.wait_ge(lo_done, m + n + 1)
                    pe.wait_ge(hi_done, m + n + 1)
                    hi, lo, dst = pT_hi[:, m % PT, c0:c1], pT_lo[:, m % PT, c0:c1], c_bank(g)[:, c0:c1]
                    nc.tensor.matmul(dst, ctx_hi[:, kt, :], hi, start=(kt == 0), stop=False)
                    nc.tensor.matmul(dst, ctx_lo[:, kt, :], hi, start=False, stop=False)
                    last = nc.tensor.matmul(dst, ctx_hi[:, kt, :], lo, start=False,
                                            stop=(kt == KT - 1 and n == len(parts) - 1))
                last.then_inc(c_done, 1)

            def turn_w_in(n):
                turn(WIN0 + n, [turned(w_in_sb[:, 2 * n + i // 2, P * (i % 2):P * (i % 2) + P]) for i in range(4)])

            def turn_w_out(n):
                turn(WOUT0 + n, [turned(w_out_sb[:, i % 2, P * (2 * n + i // 2):P * (2 * n + i // 2) + P])
                                 for i in range(4)])

            def values(g):
                pe.wait_ge(oT_ready, g + 1)
                if g == 0:
                    pe.wait_ge(ld_wv, 16)
                    pe.wait_ge(ld_wo, 16)
                    pe.wait_ge(k_sq, UNITS * G)
                    pe.wait_ge(k_bn, UNITS * G)
                    pe.wait_ge(rkT_ready, G)
                if 0 < g:
                    pe.wait_ge(y_added, GH * g)
                for j in range(GH):
                    h = GH * g + j
                    if g == G - 1 and j == GH // 2:
                        pe.wait_ge(oT_ready, G + 1)
                    last = nc.tensor.matmul(v_home(g, j), wv[:, D * h:D * h + D], oT[:, T * j:T * j + T],
                                            start=True, stop=True)
                    if j == GH - 1 or g == G - 1 and j == GH // 2 - 1:
                        last.then_inc(vo_done, 1)

            def into_out(g):
                pe.wait_ge(voT_ready, g + 1)
                for j in range(GH):
                    h = GH * g + j
                    if g == G - 1 and j == GH // 2:
                        pe.wait_ge(voT_ready, G + 1)
                    last = nc.tensor.matmul(y_home(g, j), voT[:, j, :], wo[:, h, :], start=True, stop=True)
                    if j % 2 == 1 or g == G - 1:
                        last.then_inc(y_done, 1)

            for s in range(SLOTS):
                k, su, cu = s, s - S_AT, s - C_AT
                before_scores(s)
                for half in range(2):
                    if half == 1 and s % UNITS == R_TURN and 0 < s // UNITS <= G:
                        turn_norms(s // UNITS - 1)
                    if 0 <= cu < G * UNITS:
                        m = 2 * cu + half
                        turn_probs(m)
                        if m >= 2:
                            times_ctx(m - 2)
                    if 0 <= su < G * UNITS:
                        s_chunk(su, half)
                if k < G * UNITS:
                    k_unit(k)
                if cu >= UNITS:
                    if cu % UNITS == V_AT:
                        values(cu // UNITS - 1)
                    if cu % UNITS == V_AT + 1:
                        into_out(cu // UNITS - 1)
            times_ctx(G * KT - 2)
            times_ctx(G * KT - 1)
            pe.wait_ge(ld_win, 16)
            turn_w_in(0)
            pe.wait_ge(oT_ready, G - 1)
            turn_w_in(1)
            values(G - 1)
            into_out(G - 1)

            for n in (2, 3):
                turn_w_in(n)
            pe.wait_ge(ld_wout, 16)
            for n in range(2):
                turn_w_out(n)
            busy = w_out_sb[:, 0, :]
            keep_warm(WARM[1], busy, bank[0])
            pe.wait_ge(ln_ready, 3)
            for a in range(DA):
                nc.tensor.transpose(x_bank[a][:, 0:T], xn2[:, P * a:P * a + P], ident[:, :]).then_inc(xT_turned, 1)
            pe.wait_ge(xT_out_v, 1)
            pe.wait_ge(xT_out_a, 1)
            pe.wait_ge(pre_v, by(WIN0 + 3, "v"))
            pe.wait_ge(pre_a, by(WOUT0 + 1, "a"))
            for i in range(2):
                for dst, w0 in ((g_bank[i], DI + i * HI), (z_bank[i], i * HI)):
                    for a in range(DA):
                        last = nc.tensor.matmul(dst[:, 0:HI], x2T[:, a, :], w_inT[:, a, w0:w0 + HI],
                                                start=(a == 0), stop=(a == DA - 1))
                    last.then_inc(pr_done, 1)
            def turn_oo(i):
                pe.wait_ge(oo_ready, i + 1)
                for n in range(2):
                    last = nc.tensor.transpose(x_bank[i][:, P * n:P * n + T], oo[:, P * (2 * i + n):P * (2 * i + n) + P],
                                               ident[:, :])
                last.then_inc(ooT_done, 1)

            turn_oo(0)
            keep_warm(1, w_out_sb[:, 0, 0:DM])
            for n in range(DI // P):
                if n % 2 == 0:
                    pe.wait_ge(ooT_ready, n // 2 + 1)
                last = nc.tensor.matmul(o_bank[:, 0:DM], ooT[:, n, :], w_outT[:, n, :],
                                        start=(n == 0), stop=(n == DI // P - 1))
                if n == 0:
                    turn_oo(1)
            last.then_inc(mo_done, 1)

            keep_warm(WARM[2], busy)
            pe.wait_ge(ln_ready, 4)
            for dst in (d_bank, x_bank[0]):
                for a in range(DA):
                    last = nc.tensor.transpose(dst[:, P * a:P * a + T], xm[:, P * a:P * a + P], ident[:, :])
                last.then_inc(xT_turned, 1)
            keep_warm(1, w_out_sb[:, 0, 0:DM], gu_bank[0])
            pe.wait_ge(xT_out_a, 2)
            for a in range(DA):
                last = nc.tensor.matmul(l_bank[:, 0:E], xmT[:, a, :], rwT[:, a, :], start=(a == 0), stop=(a == DA - 1))
            last.then_inc(lg_done, 1)

            def halves_product(dst, w, m, first, last):
                (w_hi, w_lo), (m_hi, m_lo) = w, m
                nc.tensor.matmul(dst, w_hi, m_hi, start=first, stop=False)
                nc.tensor.matmul(dst, w_hi, m_lo, start=False, stop=False)
                return nc.tensor.matmul(dst, w_lo, m_hi, start=False, stop=last)

            def gate_up(e):
                if e == 0:
                    pe.wait_ge(xl_ready, 1)
                pe.wait_ge(gl_ready, e + 1)
                if e >= GU:
                    pe.wait_ge(act_ready, e - GU + 1)
                for a in range(DA):
                    last = halves_product(gu_bank[e % GU][:, 0:2 * I], (xmT_hi[:, a, :], xmT_lo[:, a, :]),
                                          (gu_hi[e % WS][:, a, :], gu_lo[e % WS][:, a, :]), a == 0, a == DA - 1)
                last.then_inc(gu_done, 1)

            def turn_acts(e):
                pe.wait_ge(act_ready, e + 1)
                if e >= 2:
                    pe.wait_ge(al_ready, e - 1)
                for a in range(2):
                    last = nc.tensor.transpose(a_bank[e % 2][0:IH, T * a:T * a + T], acts[:, e % AD, IH * a:IH * a + IH],
                                               ident[:, :])
                last.then_inc(at_done, 1)

            def down(e):
                pe.wait_ge(al_ready, e + 1)
                pe.wait_ge(dl_ready, e + 1)
                for a in range(2):
                    last = halves_product(d_bank[:, 0:DM], (actT_hi[:, e % 2, a, :], actT_lo[:, e % 2, a, :]),
                                          (dw_hi[:, e % DS, a, :], dw_lo[:, e % DS, a, :]),
                                          e == 0 and a == 0, e == E - 1 and a == 1)
                last.then_inc(dn_done, 1)

            for e in range(E + TL + 1):
                if e < E:
                    gate_up(e)
                if TL <= e < E + TL:
                    turn_acts(e - TL)
                if e > TL:
                    down(e - TL - 1)

        @block.scalar
        def _(act):
            act.dma_start(wk_sb[:, 0:BANK], Wk[:, 0:BANK]).then_inc(ld_wk[0], 16)

            def wk_half(i):
                act.wait_ge(ld_wk[min(i, 1)], 16)
                nc.scalar.activation(wk_hi[:, i * BANK:i * BANK + BANK], wk_sb[:, i * BANK:i * BANK + BANK],
                                     ACT.Copy).then_inc(wk_hi_done, 1)

            def ctx_half(i):
                act.wait_ge(pre_t, i + 1)
                nc.scalar.activation(ctxT_hi[:, i * BANK:i * BANK + BANK], pre_bank[i % 2][:, :],
                                     ACT.Copy).then_inc(pre_a, 1)

            ctx_half(0)
            wk_half(0)
            ctx_half(1)
            ctx_half(2)

            def emptied(n, dst, scale=1.0, cols=BANK):
                act.wait_ge(pre_t, n + 1)
                src = pre_bank[n % 2][0:dst.shape[0], 0:cols]
                nc.scalar.activation(dst, src, ACT.Copy, scale=scale).then_inc(pre_a, 1)

            def flat(ap):
                return ap.rearrange("p a b -> p (a b)")

            def before_scores(s):
                if s == 1:
                    ctx_half(3)
                if s == 3:
                    emptied(XN, flat(xnT[:, :, :]), cols=DM)
                if s in WK_AT:
                    wk_half(WK_AT.index(s) + 1)
                if 4 <= s < 8:
                    for h in range(GH * (s - 4), GH * (s - 3)):
                        act.wait_ge(q_copied, h // 4 + 1)
                        if h >= 4:
                            act.wait_ge(q_sq, h - 3)
                        nc.scalar.activation(junk_a[:, h % 4, :], q_bank[h // 4 % 2][:, D * (h % 4):D * (h % 4) + D],
                                             ACT.Square, accum_out=qsq[:, h:h + 1]).then_inc(q_sq, 1)
                if s in (11, 12):
                    act.wait_ge(gg_ready, 1)
                    for n in (2 * s - 22, 2 * s - 21):
                        emptied(QT0 + n, flat(qT[:, 4 * n:4 * n + 4, :]), scale=gg_s[:, 0:1])
                if s in (8, 10):
                    n = s - 7
                    emptied(WK0 + n, flat(wkT[:, 4 * n:4 * n + 4, :]))
                if s in (13, 14):
                    for n in (2 * s - 26, 2 * s - 25):
                        emptied(U0 + n, flat(u_hi[:, 4 * n:4 * n + 4, :]))
                if s == 15:
                    act.wait_ge(pre_t, RW0 + 1)
                    nc.scalar.activation(rwT[:, :, :],
                                         pre_bank[RW0 % 2][:, 0:2 * P].rearrange("p (a e) -> p a e", a=2)[:, :, 0:E],
                                         ACT.Copy).then_inc(pre_a, 1)

            def exp_head(h):
                act.wait_ge(nmax_ready, h + 1)
                row = prob[(h // GH) % 2][:, h % GH, :]
                nc.scalar.activation(row, row, ACT.Exp, bias=nmax[:, h:h + 1],
                                     accum_out=psum_[:, h:h + 1]).then_inc(p_ready, 1)

            def exp_last(n):
                act.wait_ge(nmax_ready, H)
                row = prob[(G - 1) % 2][:, GH - 1, n * NKEY // EXP_PARTS:(n + 1) * NKEY // EXP_PARTS]
                nc.scalar.activation(row, row, ACT.Exp, bias=nmax[:, H - 1:H],
                                     accum_out=psum_[:, H + n:H + n + 1]).then_inc(p_ready, 1)

            def leave_ctx(g, c0=0, c1=2 * HALF):
                act.wait_ge(c_done, KT * (g + 1))
                if g == 0:
                    act.wait_ge(k_done, G * KT)
                if g > 0:
                    act.wait_ge(vo_done, g)
                nc.scalar.activation(oT[:, c0:c1], c_bank(g)[:, c0:c1], ACT.Copy).then_inc(oT_ready, 1)

            def leave_value(g):
                act.wait_ge(vo_done, g + 1)
                if g > 0:
                    act.wait_ge(y_done, 2 * g)
                nc.scalar.activation(flat(voT[:, :, :]), bank[0][:, :], ACT.Copy).then_inc(voT_ready, 1)

            def norms_out(g):
                act.wait_ge(rk_turned, g + 1)
                if g > 0:
                    act.wait_ge(rrow_ld, 16 * GH * g)
                nc.scalar.activation(rkT[:, :], norm_bank(g)[0:GH * KT, 0:P], ACT.Copy).then_inc(rkT_ready, 1)

            def gate_up_high(e):
                if e in FIRST_OF:
                    act.wait_ge(ld_exp[FIRST_OF[e]], 64)
                if e >= WS:
                    act.wait_ge(gu_done, e - WS + 1)
                nc.scalar.activation(flat(gu_hi[e % WS][:, :, :]), gu_loaded(e), ACT.Copy).then_inc(gh_ready, 1)

            for s in range(SLOTS):
                k, su, cu = s, s - S_AT, s - C_AT
                before_scores(s)
                for half in range(2):
                    if 0 <= cu < G * UNITS:
                        m = 2 * cu + half
                        act.wait_ge(t_done, m + 1)
                        if m >= PT:
                            act.wait_ge(c_done, m - PT + 1)
                        if m < G * KT - 1:
                            nc.scalar.activation(pT_hi[:, m % PT, :], t_bank[m % 2][:, :], ACT.Copy).then_inc(hi_done, 1)
                        else:
                            nc.scalar.activation(pT_hi[:, m % PT, 0:HALF], t_bank[m % 2][:, 0:HALF],
                                                 ACT.Copy).then_inc(hi_done, 1)
                            act.wait_ge(t_done, m + 2)
                            nc.scalar.activation(pT_hi[:, m % PT, HALF:], bank[3][:, 0:HALF], ACT.Copy).then_inc(hi_done, 1)
                        if m % KT == 1 and m > KT:
                            leave_ctx(m // KT - 1)
                    if half == 1 and su > 0 and su % 2 == 0 and su < G * UNITS:
                        exp_head(su // 2 - 1)
                    if G * UNITS <= su < G * UNITS + EXP_PARTS // 2:
                        exp_last(2 * (su - G * UNITS) + half)
                    if half == 1 and s % UNITS == R_TURN and 0 < s // UNITS <= G:
                        norms_out(s // UNITS - 1)
                if k < G * UNITS:
                    g, t = k // UNITS, 2 * (k % UNITS)
                    act.wait_ge(k_done, KT * g + t + 1)
                    for j in range(GH):
                        kj = k_home(KT * g + t)[:, D * j:D * j + D]
                        last = nc.scalar.activation(kj, kj, ACT.Square, accum_out=ssq[:, g, j, t:t + 1])
                    last.then_inc(k_sq, 1)
                if cu >= UNITS and cu % UNITS == V_AT:
                    leave_value(cu // UNITS - 1)
                if s in E_AT:
                    gate_up_high(E_AT.index(s))
                if s == G * UNITS + 11:
                    act.wait_ge(dt_neg, 1)
                    nc.scalar.activation(dt_sb[:, :], dt_sb[:, :], ACT.Exp, bias=dstat[:, 0:1], scale=-1.0,
                                         accum_out=dstat[:, 1:2]).then_inc(dt_exp, 1)
                    nc.scalar.activation(dt_c[:, :], dt_c[:, :], ACT.Exp, bias=dstat[:, 0:1], scale=-1.0).then_inc(dt_exp, 1)
            def w_in_out(n):
                act.wait_ge(pre_t, WIN0 + n + 1)
                nc.scalar.activation(w_in_place(n), w_in_turned(n), ACT.Copy).then_inc(pre_a, 1)

            for n in range(2):
                leave_ctx(G - 1, n * HALF, n * HALF + HALF)
            w_in_out(0)
            act.wait_ge(y_done, 2 * (G - 1))
            for n in range(2):
                act.wait_ge(vo_done, G + n)
                nc.scalar.activation(flat(voT[:, 2 * n:2 * n + 2, :]), bank[(0, 5)[n]][:, 0:HALF],
                                     ACT.Copy).then_inc(voT_ready, 1)

            nc.scalar.preload_act_table(ACT.Sigmoid)
            for n in (2, 3):
                w_in_out(n)
            act.wait_ge(y_done, Y_ALL)
            gate_up_high(EW)
            act.wait_ge(dtw_ready, 1)
            for n in range(2):
                act.wait_ge(pre_t, WOUT0 + n + 1)
                for i in (2 * n, 2 * n + 1):
                    last = nc.scalar.activation(w_outT[:, i, :], pre_bank[(WOUT0 + n) % 2][:, DM * (i % 2):DM * (i % 2) + DM],
                                                ACT.Copy, scale=dt_c[:, i:i + 1])
                last.then_inc(pre_a, 1)
            gate_up_high(EW + 1)
            act.wait_ge(xT_turned, 2)
            act.wait_ge(ld_gb, 64)
            nc.scalar.activation(x2T[:, 1, :], x_bank[1][:, 0:T], ACT.Identity, bias=beta_c[:, 1:2],
                                 scale=gamma_c[:, 1:2]).then_inc(xT_out_a, 1)
            for i in range(2):
                for k in (1, 0):
                    act.wait_ge(clip_done, 2 * i + 2 - k)
                    nc.scalar.activation(sg[:, k, i * HI:i * HI + HI], zc[:, k, i * HI:i * HI + HI],
                                         ACT.Sigmoid).then_inc(sig_done, 1)
            for i in range(2):
                act.wait_ge(ooT_done, i + 1)
                nc.scalar.activation(flat(ooT[:, 2 * i:2 * i + 2, :]), x_bank[i][:, 0:2 * P], ACT.Copy).then_inc(ooT_ready, 1)
            nc.scalar.preload_act_table(ACT.Exp)
            for e in range(EW + 2, WS):
                gate_up_high(e)
            act.wait_ge(xT_turned, 3)
            nc.scalar.activation(flat(xmT_hi[:, :, :]), d_bank[:, 0:DM], ACT.Copy).then_inc(xh_ready, 1)
            act.wait_ge(xT_turned, 4)
            nc.scalar.activation(flat(xmT[:, :, :]), x_bank[0][:, 0:DM], ACT.Copy).then_inc(xT_out_a, 1)
            act.wait_ge(lg_max, 1)
            nc.scalar.activation(ex[:, :], lg[:, :], ACT.Exp, bias=lstat[:, 1:2]).then_inc(lg_exp, 1)
            nc.scalar.preload_act_table(ACT.Silu)
            for e in range(E + TL):
                if e >= TL:
                    i = e - TL
                    act.wait_ge(at_done, i + 1)
                    if i >= 2:
                        act.wait_ge(dn_done, i - 1)
                    nc.scalar.activation(flat(actT_hi[:, i % 2, :, :]), a_bank[i % 2][0:IH, 0:2 * T],
                                         ACT.Copy).then_inc(ah_ready, 1)
                if e < E:
                    act.wait_ge(gu_done, e + 1)
                    if e >= 2:
                        act.wait_ge(act_ready, e - 1)
                    nc.scalar.activation(silu_g[:, e % 2, :], gu_bank[e % GU][:, 0:I], ACT.Silu).then_inc(silu_done, 1)
                if e + WS < E:
                    gate_up_high(e + WS)

        @block.vector
        def _(dve):
            steps = [0]

            def link(ins):
                steps[0] += 1
                ins.then_inc(dve_seq, 1)
                dve.wait_ge(dve_seq, steps[0])

            def first_rsqrt(y, v):
                link(nc.vector.tensor_scalar(out=y.bitcast(I32), in0=v.bitcast(I32), scalar1=1, scalar2=None,
                                             op0=ALU.logical_shift_right))
                nc.vector.tensor_scalar(out=y.bitcast(I32), in0=y.bitcast(I32), scalar1=-1.0,
                                        scalar2=float(0x5F3759DF), op0=ALU.mult, op1=ALU.add).then_inc(guess_ready, 1)

            def ln_stats(n, src):
                link(nc.vector.bn_stats(out=stat[:, :], in_=src))
                link(nc.vector.bn_aggr(out=mv[:, :], in_=stat[:, :]))
                nc.vector.tensor_scalar(out=mv[:, 1:2], in0=mv[:, 1:2], scalar1=EPS, scalar2=None,
                                        op0=ALU.add).then_inc(var_ready, 1)

            def normed(dst, src):
                return nc.vector.tensor_scalar(out=dst, in0=src, scalar1=mv[:, 0:1], scalar2=rstd[:, 0:1],
                                               op0=ALU.subtract, op1=ALU.mult)

            def flat(ap):
                return ap.rearrange("p a b -> p (a b)")

            def wk_low(i):
                c0 = slice(i * BANK, i * BANK + BANK)
                dve.wait_ge(wk_hi_done, i + 1)
                nc.vector.tensor_tensor(out=wk_lo[:, c0], in0=wk_sb[:, c0], in1=wk_hi[:, c0].bitcast(F32),
                                        op=ALU.subtract).then_inc(wk_lo_done, 1)

            def ctx_low(i):
                c0 = slice(i * BANK, i * BANK + BANK)
                dve.wait_ge(pre_a, i + 1)
                nc.vector.tensor_tensor(out=ctxT_lo[:, c0], in0=pre_bank[i % 2][:, :],
                                        in1=ctxT_hi[:, c0].bitcast(F32), op=ALU.subtract).then_inc(pre_v, 1)

            ctx_low(0)
            wk_low(0)
            ctx_low(1)
            ctx_low(2)

            def before_scores(s):
                if s == 0:
                    dve.wait_ge(ld_x, 16)
                    dve.wait_ge(mhalf_made, 1)
                    ln_stats(0, x_sb[:, :])
                if s == 1:
                    ctx_low(3)
                    dve.wait_ge(rstd_ready, 1)
                    normed(xn[:, :], x_sb[:, :]).then_inc(ln_ready, 1)
                if s in WK_AT:
                    wk_low(WK_AT.index(s) + 1)
                if 4 <= s < 8:
                    n = s - 4
                    dve.wait_ge(q_done, n + 1)
                    nc.vector.tensor_copy(q_sb[:, n * BANK:n * BANK + BANK], q_bank[n % 2][:, :]).then_inc(q_copied, 1)
                if s == 8:
                    dve.wait_ge(ld_g, 32)
                    nc.vector.scalar_tensor_tensor(out=gg_s[:, :], in0=gcol[:, 0:1], scalar=float(D) ** -0.5,
                                                   in1=gcol[:, 1:2], op0=ALU.mult, op1=ALU.mult).then_inc(gg_ready, 1)
                    dve.wait_ge(q_sq, H)
                    link(nc.vector.tensor_scalar(out=qsq[:, :], in0=qsq[:, :], scalar1=1.0 / D, scalar2=EPS,
                                                 op0=ALU.mult, op1=ALU.add))
                    first_rsqrt(rq[:, :], qsq[:, :])
                if s in (8, 10):
                    n = s - 8
                    emptied(WK0 + n, flat(wkT[:, 4 * n:4 * n + 4, :]), pre_bank[(WK0 + n) % 2][:, :])
                if s in (10, 11):
                    dve.wait_ge(rq_ready, 1)
                    for n in (2 * s - 20, 2 * s - 19):
                        q4 = q_sb[:, n * BANK:n * BANK + BANK].rearrange("p (h d) -> p h d", d=D)
                        nc.vector.tensor_tensor(
                            out=q4, in0=q4, in1=rq[:, 4 * n:4 * n + 4].unsqueeze(2).to_broadcast([T, 4, D]),
                            op=ALU.mult).then_inc(q_norm, 1)
                if s in (13, 14):
                    for n in (2 * s - 26, 2 * s - 25):
                        dve.wait_ge(pre_a, by(U0 + n, "a"))
                        nc.vector.tensor_tensor(out=flat(u_lo[:, 4 * n:4 * n + 4, :]), in0=pre_bank[(U0 + n) % 2][:, :],
                                                in1=flat(u_hi[:, 4 * n:4 * n + 4, :]).bitcast(F32),
                                                op=ALU.subtract).then_inc(pre_v, 1)

            def emptied(n, dst, src):
                dve.wait_ge(pre_t, n + 1)
                nc.vector.tensor_copy(dst, src).then_inc(pre_v, 1)

            def k_stats(k):
                g, t = k // UNITS, 2 * (k % UNITS) + 1
                dve.wait_ge(k_done, KT * g + t + 1)
                if g > 1 and t == 1:
                    dve.wait_ge(kv_ready, g - 1)
                for j in range(GH):
                    last = nc.vector.bn_stats(out=bn[:, g % 2, j, t // 2, :], in_=k_home(KT * g + t)[:, D * j:D * j + D])
                last.then_inc(k_bn, 1)

            def first_key_norms(g):
                dve.wait_ge(kv_ready, g + 1)
                first_rsqrt(rk[:, g, :, :].rearrange("p h t -> p (h t)"), ssq[:, g, :, :].rearrange("p h t -> p (h t)"))

            def scaled_scores(u, c2):
                h, c = u // 2, 2 * (u % 2) + c2
                n = NC * h + c
                g, j = h // GH, h % GH
                dve.wait_ge(s_done, n + 1)
                dve.wait_ge(rbc_ready, h + 1)
                if j == 0 and g >= 2:
                    dve.wait_ge(t_done, KT * (g - 2) + (c + 1) * BANK // P)
                c0 = slice(c * BANK, c * BANK + BANK)
                nc.vector.tensor_tensor_reduce(out=prob[g % 2][:, j, c0], in0=s_bank[n % 3][:, :],
                                               in1=rbc[h % 2][:, c0], scale=1.0, scalar=-3.0e38, op0=ALU.mult,
                                               op1=ALU.max, accum_out=smax[:, h, c:c + 1]).then_inc(sr_done, 1)
                if c == NC - 1:
                    dve.wait_ge(sr_done, n + 1)
                    link(nc.vector.tensor_reduce(out=pmax[:, h:h + 1], in_=smax[:, h, :], axis=AX.X, op=ALU.max))
                    nc.vector.tensor_scalar(out=nmax[:, h:h + 1], in0=pmax[:, h:h + 1], scalar1=-1.0, scalar2=None,
                                            op0=ALU.mult).then_inc(nmax_ready, 1)

            def over_sums(g):
                dve.wait_ge(p_ready, GH * (g + 1) + (EXP_PARTS - 1 if g == G - 1 else 0))
                if g == G - 1:
                    link(nc.vector.tensor_reduce(out=psum_[:, H - 1:H], in_=psum_[:, H:H + EXP_PARTS], axis=AX.X,
                                                 op=ALU.add))
                link(nc.vector.reciprocal(out=rs[:, GH * g:GH * g + GH], in_=psum_[:, GH * g:GH * g + GH]))

            def add_head(h):
                g, j = h // GH, h % GH
                dve.wait_ge(y_done, y_count(g, j))
                if h > 0:
                    dve.wait_ge(y_added, h)
                nc.vector.scalar_tensor_tensor(out=x1[:, :], in0=y_home(g, j), scalar=rs[:, h:h + 1],
                                               in1=(x_sb if h == 0 else x1)[:, :], op0=ALU.mult,
                                               op1=ALU.add).then_inc(y_added, 1)

            def gate_up_low(e):
                if e == EW:
                    dve.wait_ge(y_done, Y_ALL)
                dve.wait_ge(gh_ready, e + 1)
                if e >= WS:
                    dve.wait_ge(gu_done, e - WS + 1)
                nc.vector.tensor_tensor(out=flat(gu_lo[e % WS][:, :, :]), in0=gu_loaded(e),
                                        in1=flat(gu_hi[e % WS][:, :, :]).bitcast(F32),
                                        op=ALU.subtract).then_inc(gl_ready, 1)

            for s in range(SLOTS):
                k, su, cu = s, s - S_AT, s - C_AT
                before_scores(s)
                for half in range(2):
                    if 0 <= cu < G * UNITS:
                        m = 2 * cu + half
                        dve.wait_ge(hi_done, m + 1)
                        if m < G * KT - 1:
                            nc.vector.tensor_tensor(out=pT_lo[:, m % PT, :], in0=t_bank[m % 2][:, :],
                                                    in1=pT_hi[:, m % PT, :].bitcast(F32),
                                                    op=ALU.subtract).then_inc(lo_done, 1)
                        else:
                            nc.vector.tensor_tensor(out=pT_lo[:, m % PT, 0:HALF], in0=t_bank[m % 2][:, 0:HALF],
                                                    in1=pT_hi[:, m % PT, 0:HALF].bitcast(F32),
                                                    op=ALU.subtract).then_inc(lo_done, 1)
                            dve.wait_ge(hi_done, m + 2)
                            nc.vector.tensor_tensor(out=pT_lo[:, m % PT, HALF:], in0=bank[3][:, 0:HALF],
                                                    in1=pT_hi[:, m % PT, HALF:].bitcast(F32),
                                                    op=ALU.subtract).then_inc(lo_done, 1)
                    if 0 <= su < G * UNITS:
                        scaled_scores(su, half)
                    if cu >= UNITS and cu % UNITS in (V_AT + 2, V_AT + 3):
                        add_head(GH * (cu // UNITS - 1) + 2 * (cu % UNITS - V_AT - 2) + half)
                if k < G * UNITS:
                    k_stats(k)
                if s % UNITS == (N_AT if s >= S_AT else N_AT + 1) and 0 < s // UNITS <= G:
                    first_key_norms(s // UNITS - 1)
                if s == G * UNITS + 8:
                    dve.wait_ge(ld_dt, 16 * (1 + DI // P))
                    nc.vector.tensor_reduce(out=dstat[:, 0:1], in_=dt_sb[:, :], axis=AX.X,
                                            op=ALU.min).then_inc(dt_neg, 1)
                if s == G * UNITS + 12:
                    dve.wait_ge(dt_exp, 2)
                    link(nc.vector.reciprocal(out=dstat[:, 2:3], in_=dstat[:, 1:2]))
                    nc.vector.tensor_scalar(out=dt_c[:, :], in0=dt_c[:, :], scalar1=dstat[:, 2:3], scalar2=None,
                                            op0=ALU.mult).then_inc(dtw_ready, 1)
                if cu >= UNITS and cu % UNITS == V_AT:
                    over_sums(cu // UNITS - 1)
                if s in E_AT:
                    gate_up_low(E_AT.index(s))
            over_sums(G - 1)
            dve.wait_ge(c_done, G * KT)
            emptied(WIN0 + 1, w_in_place(1), w_in_turned(1))
            for h in range(H - GH, H):
                add_head(h)

            dve.wait_ge(y_added, H)
            ln_stats(1, x1[:, :])
            dve.wait_ge(rstd_ready, 2)
            normed(y1[:, :], x1[:, :]).then_inc(ln_ready, 1)
            dve.wait_ge(ln_ready, 2)
            ln_stats(2, y1[:, :])
            dve.wait_ge(rstd_ready, 3)
            normed(xn2[:, :], y1[:, :]).then_inc(ln_ready, 1)
            nc.vector.tensor_tensor(out=s1[:, :], in0=x1[:, :], in1=y1[:, :], op=ALU.add).then_inc(s1_ready, 1)
            dve.wait_ge(xT_turned, 1)
            dve.wait_ge(ld_gb, 64)
            nc.vector.tensor_scalar(out=x2T[:, 0, :], in0=x_bank[0][:, 0:T], scalar1=gamma_c[:, 0:1],
                                    scalar2=beta_c[:, 0:1], op0=ALU.mult, op1=ALU.add).then_inc(xT_out_v, 1)
            gate_up_low(EW)
            def clipped(i, k):
                dve.wait_ge(pr_done, 2 * i + 2 - k)
                nc.vector.tensor_scalar(out=zc[:, k, i * HI:i * HI + HI], in0=(z_bank, g_bank)[k][i][:, 0:HI],
                                        scalar1=15.0, scalar2=-15.0, op0=ALU.min, op1=ALU.max).then_inc(clip_done, 1)

            def gate_part(i):
                c0 = slice(i * HI, i * HI + HI)
                dve.wait_ge(clip_done, 2 * i + 1)
                dve.wait_ge(sig_done, 2 * i + 1)
                nc.vector.tensor_tensor(out=gg[:, c0], in0=zc[:, 1, c0], in1=sg[:, 1, c0], op=ALU.mult).then_inc(gg_done, 1)

            def z_part(i):
                c0 = slice(i * HI, i * HI + HI)
                dve.wait_ge(gg_done, i + 1)
                link(nc.vector.tensor_tensor(out=zz[:, c0], in0=z_bank[i][:, 0:HI], in1=gg[:, c0], op=ALU.mult))
                dve.wait_ge(sig_done, 2 * i + 2)
                nc.vector.tensor_tensor(out=oo[:, c0], in0=zz[:, c0], in1=sg[:, 0, c0], op=ALU.mult).then_inc(oo_ready, 1)

            clipped(0, 1)
            clipped(0, 0)
            gate_part(0)
            clipped(1, 1)
            z_part(0)
            clipped(1, 0)
            gate_part(1)
            z_part(1)
            gate_up_low(EW + 1)
            dve.wait_ge(s1_ready, 1)
            dve.wait_ge(mo_done, 1)
            link(nc.vector.tensor_tensor(out=x2[:, :], in0=o_bank[:, 0:DM], in1=s1[:, :], op=ALU.add))
            ln_stats(3, x2[:, :])
            dve.wait_ge(rstd_ready, 4)
            normed(xm[:, :], x2[:, :]).then_inc(ln_ready, 1)
            for e in range(EW + 2, WS):
                gate_up_low(e)

            dve.wait_ge(xh_ready, 1)
            nc.vector.tensor_tensor(out=flat(xmT_lo[:, :, :]), in0=d_bank[:, 0:DM],
                                    in1=flat(xmT_hi[:, :, :]).bitcast(F32), op=ALU.subtract).then_inc(xl_ready, 1)

            dve.wait_ge(lg_done, 1)
            dve.wait_ge(ld_bias, 16)
            link(nc.vector.tensor_tensor_reduce(out=lg[:, :], in0=l_bank[:, 0:E], in1=bias_bc[:, :], scale=1.0,
                                                scalar=-3.0e38, op0=ALU.add, op1=ALU.max, accum_out=lstat[:, 0:1]))
            nc.vector.tensor_scalar(out=lstat[:, 1:2], in0=lstat[:, 0:1], scalar1=-1.0, scalar2=None,
                                    op0=ALU.mult).then_inc(lg_max, 1)
            dve.wait_ge(before_made, 2)
            other = lg[:, :].unsqueeze(1).to_broadcast([T, E, E])
            own = lg[:, :].unsqueeze(2).to_broadcast([T, E, E])
            link(nc.vector.tensor_tensor(out=cmp_a[:, :, :], in0=other, in1=own, op=ALU.subtract))
            link(nc.vector.scalar_tensor_tensor(out=cmp_b[:, :, :], in0=cmp_a[:, :, :], scalar=0.0, in1=before[:, :, :],
                                                op0=ALU.is_equal, op1=ALU.mult))
            link(nc.vector.scalar_tensor_tensor(out=cmp_b[:, :, :], in0=cmp_a[:, :, :], scalar=0.0, in1=cmp_b[:, :, :],
                                                op0=ALU.is_gt, op1=ALU.add))
            link(nc.vector.tensor_reduce(out=rank[:, :], in_=cmp_b[:, :, :], axis=AX.X, op=ALU.add))
            dve.wait_ge(lg_exp, 1)
            link(nc.vector.scalar_tensor_tensor(out=top[:, :], in0=rank[:, :], scalar=float(TOP_K), in1=ex[:, :],
                                                op0=ALU.is_lt, op1=ALU.mult))
            for e in range(E + TL):
                if e >= TL:
                    i = e - TL
                    dve.wait_ge(ah_ready, i + 1)
                    nc.vector.tensor_tensor(out=flat(actT_lo[:, i % 2, :, :]), in0=a_bank[i % 2][0:IH, 0:2 * T],
                                            in1=flat(actT_hi[:, i % 2, :, :]).bitcast(F32),
                                            op=ALU.subtract).then_inc(al_ready, 1)
                if e < E:
                    dve.wait_ge(silu_done, e + 1)
                    if e >= AD:
                        dve.wait_ge(at_done, e - AD + 1)
                    nc.vector.scalar_tensor_tensor(out=acts[:, e % AD, :], in0=silu_g[:, e % 2, :],
                                                   scalar=top[:, e:e + 1], in1=gu_bank[e % GU][:, I:2 * I],
                                                   op0=ALU.mult, op1=ALU.mult).then_inc(act_ready, 1)
                if e == LL:
                    link(nc.vector.tensor_reduce(out=lstat[:, 2:3], in_=top[:, :], axis=AX.X, op=ALU.add))
                    link(nc.vector.reciprocal(out=lstat[:, 3:4], in_=lstat[:, 2:3]))
                if LL <= e and e - LL + WS < E:
                    gate_up_low(e - LL + WS)
            dve.wait_ge(dn_done, E)
            nc.vector.scalar_tensor_tensor(out=x3[:, :], in0=d_bank[:, 0:DM], scalar=lstat[:, 3:4], in1=x2[:, :],
                                           op0=ALU.mult, op1=ALU.add).then_inc(x3_ready, 1)


_INS = ['x', 'ctx_1024', 'L0_xattn_Wq', 'L0_xattn_Wk', 'L0_xattn_Wv', 'L0_xattn_Wo', 'L0_xattn_gq', 'L0_xattn_gk',
        'L0_attn_gamma', 'L0_attn_beta', 'L0_attn_W_in', 'L0_attn_W_out', 'L0_attn_dt', 'L0_ffn_router_w',
        'L0_ffn_expert_bias', 'L0_ffn_gate_proj', 'L0_ffn_up_proj', 'L0_ffn_down_proj']


def kernel(**inputs):
    import numpy as _np
    import concourse.bacc as _bacc
    from concourse import mybir as _mybir
    from concourse.bass_utils import run_bass_kernel_spmd as _run

    nc = _bacc.Bacc("TRN2", target_bir_lowering=False, num_devices=1)
    arrays, args = {}, []
    for name in _INS:
        a = _np.ascontiguousarray(inputs[name])
        arrays[f"in_{name}"] = a
        args.append(nc.dram_tensor(f"in_{name}", a.shape, _mybir.dt.from_np(a.dtype), kind="ExternalInput").ap())
    shape = inputs['x'].shape
    args.append(nc.dram_tensor("out_0", shape, _mybir.dt.float32, kind="ExternalOutput").ap())
    perceiver_layer(nc, *args)
    r = _run(nc, [arrays], core_ids=[0])
    return r.results[0]["out_0"]
```
